# Optimizing a Trainium2 kernel written in Bass

```python
import numpy as np
import jax
import jax.numpy as jnp

def _softmax(x, axis=-1):
    return jax.nn.softmax(x, axis=axis)

def _gelu(x):
    return jax.nn.gelu(x, approximate=True)

def _silu(x):
    return jax.nn.silu(x)

def _sigmoid(x):
    return jax.nn.sigmoid(x)

def _layernorm(x, axis=-1, eps=1e-05):
    m = jnp.mean(x, axis=axis, keepdims=True)
    v = jnp.var(x, axis=axis, keepdims=True)
    return (x - m) / jnp.sqrt(v + eps)

def _scatter_add(tgt, idx, src, axis=0):
    return tgt.at[idx].add(src)

def _segment_sum(src, seg, n):
    return jax.ops.segment_sum(src, seg, n)
kernel_name = 'mk_seq_postln_d1_jaxref_r4_d6ad85'

def setup_inputs(seed: int=0):
    np.random.seed(seed)
    _w = jnp.asarray

    def _L0_attn_setup():
        import jax, jax.numpy as jnp
        import numpy as np
        B, S, D = (8, 512, 256)
        key = jax.random.key(seed)
        kx, kw, kb = jax.random.split(key, 3)
        x = jax.random.normal(kx, (B, S, D), dtype=jnp.float32)
        W = jax.random.normal(kw, (3 * D, D), dtype=jnp.float32) * (1.0 / np.sqrt(D))
        b = jax.random.normal(kb, (3 * D,), dtype=jnp.float32) * 0.01
        return {'x': x, 'W': W, 'b': b}
    _L0_attn_in = _L0_attn_setup()

    def _L0_ffn_setup():
        import jax, jax.numpy as jnp
        import numpy as np
        EMB = 256
        FF = 4 * EMB

        def _ternary(w):
            scale = jnp.maximum(jnp.mean(jnp.abs(w)), 1e-08)
            w_t = jnp.clip(jnp.round(w / scale), -1.0, 1.0)
            return w + jax.lax.stop_gradient(w_t - w)
        key = jax.random.key(seed)
        kx, k1, k2, kb1, kb2 = jax.random.split(key, 5)
        x = jax.random.normal(kx, (4, 512, EMB), dtype=jnp.float32)
        lim1 = 1.0 / np.sqrt(EMB)
        lim2 = 1.0 / np.sqrt(FF)
        W1 = jax.random.uniform(k1, (FF, EMB), jnp.float32, -lim1, lim1)
        b1 = jax.random.uniform(kb1, (FF,), jnp.float32, -lim1, lim1)
        W2 = jax.random.uniform(k2, (EMB, FF), jnp.float32, -lim2, lim2)
        b2 = jax.random.uniform(kb2, (EMB,), jnp.float32, -lim2, lim2)
        return {'x': x, 'W1': W1, 'b1': b1, 'W2': W2, 'b2': b2}
    _L0_ffn_in = _L0_ffn_setup()
    _d = {'L0_attn_x': _L0_attn_in['x'], 'L0_attn_W': _L0_attn_in['W'], 'L0_attn_b': _L0_attn_in['b'], 'L0_ffn_W1': _L0_ffn_in['W1'], 'L0_ffn_b1': _L0_ffn_in['b1'], 'L0_ffn_W2': _L0_ffn_in['W2'], 'L0_ffn_b2': _L0_ffn_in['b2']}
    _x0 = _d['L0_attn_x']
    _d['L0_attn_x'] = jax.random.normal(jax.random.fold_in(jax.random.key(seed), 1), (8, 1024, 256), dtype=_x0.dtype)
    del _x0
    return _d

def reference(L0_attn_x, L0_attn_W, L0_attn_b, L0_ffn_W1, L0_ffn_b1, L0_ffn_W2, L0_ffn_b2):

    def _L0_attn_ref(x, W, b):
        import jax, jax.numpy as jnp
        import numpy as np
        B, S, D = (8, 512, 256)
        qkv = jnp.einsum('bsd,fd->bsf', x, W) + b
        q, k, v = jnp.split(qkv, 3, axis=-1)
        attn = jnp.einsum('bik,bjk->bij', q, k) / k.shape[-1]
        attn = jax.nn.softmax(attn, axis=1)
        out = jnp.einsum('bij,bjk->bik', attn, v)
        return out

    def _L0_ffn_ref(x, W1, b1, W2, b2):
        import jax, jax.numpy as jnp
        import numpy as np
        EMB = 256
        FF = 4 * EMB

        def _ternary(w):
            scale = jnp.maximum(jnp.mean(jnp.abs(w)), 1e-08)
            w_t = jnp.clip(jnp.round(w / scale), -1.0, 1.0)
            return w + jax.lax.stop_gradient(w_t - w)
        h = jnp.einsum('bsd,fd->bsf', x, _ternary(W1)) + b1
        h = jax.nn.gelu(h, approximate=False)
        out = jnp.einsum('bsf,df->bsd', h, _ternary(W2)) + b2
        return out
    x = L0_attn_x
    x = _layernorm(x + _L0_attn_ref(x, L0_attn_W, L0_attn_b), axis=-1)
    x = _layernorm(x + _L0_ffn_ref(x, L0_ffn_W1, L0_ffn_b1, L0_ffn_W2, L0_ffn_b2), axis=-1)
    return x

_drawn_inputs = setup_inputs


def setup_inputs(seed=0):
    import zlib

    import numpy as np

    out = dict(_drawn_inputs(seed))
    spreads = {}
    factors = {'L0_attn_b': 4.936, 'L0_ffn_b1': 23.028, 'L0_ffn_b2': 64.0}
    for name, (base, spread) in spreads.items():
        noise = np.random.default_rng([zlib.crc32(name.encode()), seed]).standard_normal(out[name].shape)
        drawn = base * np.exp(spread * noise) if base else spread * noise
        out[name] = jnp.asarray(drawn.astype(out[name].dtype))
    for name, factor in factors.items():
        out[name] = (out[name] * factor).astype(out[name].dtype)
    return out
```

```python
from contextlib import ExitStack

import concourse.bass as bass
from concourse import mybir

ALU = mybir.AluOpType
ACT = mybir.ActivationFunctionType
F32 = mybir.dt.float32
F32R = mybir.dt.float32r
AX_X = mybir.AxisListType.X

P = 128
HALF = 512
LN_EPS = 1e-5
MIN_SCALE = 1e-8
NEG, POS = 0, 1


def postln_block_kernel(nc, x, x_t, w_qk, w_v, b_q, b_k, b_v, w1_t, b1, w2_t, b2, eye, out):
    B, S, D = x.shape
    DC = D // P
    TILES = S // P
    NH = S // HALF
    TPH = HALF // P
    FF = b1.shape[0] * b1.shape[1]
    FC = FF // P
    U = NH * FC
    DV = D + 2
    SCALE = 1.0 / D
    L = 2 * TILES
    assert NH == 2 and DC == 2 and TILES == 8 and FC == 8

    with ExitStack() as ctx:
        def sb(name, shape, dt=F32):
            return ctx.enter_context(nc.sbuf_tensor(name, shape, dt))

        def ps(name, shape):
            return ctx.enter_context(nc.psum_tensor(name, shape, F32))

        def sem(name):
            return ctx.enter_context(nc.semaphore(name))

        ones = sb("ones", [P, P])
        identity = sb("identity", [P, P])
        m_hi, m_lo = sb("m_hi", [P, DC, D], F32R), sb("m_lo", [P, DC, D], F32R)
        wv_hi, wv_lo = sb("wv_hi", [P, DC, DV], F32R), sb("wv_lo", [P, DC, DV], F32R)
        w1 = sb("w1", [P, DC, FF], F32R)
        w2 = sb("w2", [P, FC, D], F32R)
        g_bias = sb("g_bias", [P, DC])
        v_bias = sb("v_bias", [P, DV])
        b1_col = sb("b1_col", [P, FC])
        b2_row = sb("b2_row", [P, D])
        bq_col, bk_col = sb("bq_col", [P, DC, 2]), sb("bk_col", [P, DC, 2])
        abs_part = sb("abs_part", [P, 2, 32])
        abs_sum = sb("abs_sum", [P, 2])
        cut = sb("cut", [P, 2, 2])
        neg_half, eps, zero = sb("neg_half", [P, 1]), sb("eps", [P, 1]), sb("zero", [P, 1])
        CONSTS = 4
        xt_raw = sb("xt_raw", [P, DC, HALF])
        xt_hi, xt_lo = sb("xt_hi", [P, DC, S], F32R), sb("xt_lo", [P, DC, S], F32R)
        x_tok = sb("x_tok", [P, 4, D])
        g_hi, g_lo = sb("g_hi", [P, DC, S], F32R), sb("g_lo", [P, DC, S], F32R)
        v_f = sb("v_f", [P, 2, DV])
        v_hi, v_lo = sb("v_hi", [P, TILES, D], F32R), sb("v_lo", [P, TILES, D], F32R)
        p_f = sb("p_f", [P, 2, S])
        p_hi, p_lo = sb("p_hi", [P, TILES, S], F32R), sb("p_lo", [P, TILES, S], F32R)
        x1 = sb("x1", [P, TILES, D])
        x1t_hi, x1t_lo = sb("x1t_hi", [P, DC, HALF], F32R), sb("x1t_lo", [P, DC, HALF], F32R)
        h_hi, h_lo = sb("h_hi", [P, FC, HALF], F32R), sb("h_lo", [P, FC, HALF], F32R)
        s_max, s_top, s_bias = sb("s_max", [P, TILES]), sb("s_top", [P, TILES]), sb("s_bias", [P, TILES])
        p_sum, p_rsum = sb("p_sum", [P, TILES]), sb("p_rsum", [P, TILES])
        stats, mean_var = sb("stats", [P, L, 6]), sb("mean_var", [P, L, 2])
        var_eps, neg_mean = sb("var_eps", [P, L]), sb("neg_mean", [P, L])
        rstd, shift = sb("rstd", [P, L]), sb("shift", [P, L])
        h_f = p_f[:].rearrange("p a (c n) -> p (a c) n", n=HALF)
        RH = 4

        ps_s = ps("ps_s", [P, 2, 2, HALF])
        ps_acc = ps("ps_acc", [P, 2, HALF])
        ps_a = ps("ps_a", [P, HALF])
        ps_b = ps("ps_b", [P, HALF])
        ps_v = [ps_a, ps_b]
        ps_h = [ps_s[:, 0, 0, :], ps_s[:, 0, 1, :], ps_b[:]]

        wqk_loaded, wv_loaded, small_loaded = sem("wqk_loaded"), sem("wv_loaded"), sem("small_loaded")
        w1_loaded, w2_loaded = sem("w1_loaded"), sem("w2_loaded")
        xt_loaded = sem("xt_loaded")
        x_loaded = [sem("x_loaded0"), sem("x_loaded1")]
        out_stored = [sem(f"out_stored{q}") for q in range(TILES // 2)]
        const_set = sem("const_set")
        bk_wide_set = sem("bk_wide_set")
        m_psum, wb_psum = sem("m_psum"), sem("wb_psum")
        m_hi_set, m_lo_set = sem("m_hi_set"), sem("m_lo_set")
        wv_hi_set, wv_lo_set, bias_set = sem("wv_hi_set"), sem("wv_lo_set"), sem("bias_set")
        abs_parts, abs_summed, abs_psum = sem("abs_parts"), sem("abs_summed"), sem("abs_psum")
        scale_set, cut_set, neg_set, tern_set = sem("scale_set"), sem("cut_set"), sem("neg_set"), sem("tern_set")
        xt_hi_set, xt_lo_set = sem("xt_hi_set"), sem("xt_lo_set")
        g_psum, g_hi_set, g_lo_set = sem("g_psum"), sem("g_hi_set"), sem("g_lo_set")
        v_psum, v_taken, v_hi_set, v_lo_set = sem("v_psum"), sem("v_taken"), sem("v_hi_set"), sem("v_lo_set")
        s_psum, max_set, top_set, bias_ready = sem("s_psum"), sem("max_set"), sem("top_set"), sem("bias_ready")
        exp_done, rsum_set = sem("exp_done"), sem("rsum_set")
        p_hi_set, p_lo_set = sem("p_hi_set"), sem("p_lo_set")
        acc_psum, acc_free = sem("acc_psum"), sem("acc_free")
        stats_set, mv_set = sem("stats_set"), sem("mv_set")
        eps_set, rstd_set, shift_set, normed = sem("eps_set"), sem("rstd_set"), sem("shift_set"), sem("normed")
        b2_added = sem("b2_added")
        t_psum, t_hi_set, t_lo_set = sem("t_psum"), sem("t_hi_set"), sem("t_lo_set")
        h_psum, gelu_done = sem("h_psum"), sem("gelu_done")
        h_hi_act, h_hi_dve, h_lo_set = sem("h_hi_act"), sem("h_hi_dve"), sem("h_lo_set")

        x_view = x.rearrange("b (p i) d -> b p i d", p=P)
        out_view = out.rearrange("b (p i) d -> b p i d", p=P)
        wq_raw, wk_raw = xt_raw[:, :, 0:D], xt_raw[:, :, D:2 * D]
        wv_raw = x_tok[:, 0:DC, :]
        w1_raw = p_f[:]
        w2_raw = x1[:]
        bk_wide = v_f[:, :, 0:P]

        block = ctx.enter_context(nc.Block())

        @block.sync
        def _(sp):
            def wait_apart(semaphore, count):
                count = count if isinstance(count, int) else sp.to_reg(count)
                sp.wait_ge(wqk_loaded, 32)
                sp.wait_ge(semaphore, count)

            def load_xt(b, half):
                sp.dma_start(xt_raw[:], x_t[b, half]).then_inc(xt_loaded, 16)

            def load_x(b, pair):
                sp.dma_start(x_tok[:, 2 * (pair % 2):2 * (pair % 2) + 2, :],
                             x_view[b, :, 2 * pair:2 * pair + 2, :]).then_inc(x_loaded[pair % 2], 16)

            def cycle(b, next_xt, next2_xt):
                if next_xt:
                    wait_apart(xt_lo_set, 2 * b + 3)
                    load_xt(b + 1, 1)
                for pair in (2, 3):
                    wait_apart(acc_free, L * b + 2 * pair)
                    load_x(b, pair)
                if next2_xt:
                    wait_apart(xt_lo_set, 2 * b + 4)
                    load_xt(b + 2, 0)
                if next_xt:
                    for pair in (0, 1):
                        wait_apart(acc_free, L * b + 2 * pair + 8)
                        load_x(b + 1, pair)
                for pair in range(TILES // 2):
                    wait_apart(normed, L * b + TILES + 2 * pair + 2)
                    sp.dma_start(out_view[b, :, 2 * pair:2 * pair + 2, :],
                                 x1[:, 2 * pair:2 * pair + 2, :]).then_inc(out_stored[pair], 16)

            sp.dma_start(wq_raw, w_qk[:, 0]).then_inc(wqk_loaded, 16)
            sp.dma_start(wk_raw, w_qk[:, 1]).then_inc(wqk_loaded, 16)
            for dst, src in ((bq_col[:], b_q), (bk_col[:], b_k), (b1_col[:], b1), (identity[:], eye),
                             (b2_row[:], b2.broadcast_to([P, D])), (v_bias[:, 0:D], b_v.broadcast_to([P, D]))):
                sp.dma_start(dst, src).then_inc(small_loaded, 16)
            sp.dma_start(wv_raw, w_v).then_inc(wv_loaded, 16)
            sp.dma_start(w1_raw, w1_t).then_inc(w1_loaded, 16)
            sp.dma_start(w2_raw, w2_t).then_inc(w2_loaded, 16)
            sp.wait_ge(m_psum, DC)
            sp.wait_ge(wb_psum, 1)
            load_xt(0, 0)
            sp.wait_ge(xt_lo_set, 1)
            load_xt(0, 1)
            sp.wait_ge(wv_lo_set, DC)
            load_x(0, 0)
            load_x(0, 1)
            sp.wait_ge(xt_lo_set, 2)
            load_xt(1, 0)
            with sp.Fori(0, B - 2) as b:
                cycle(b, True, True)
            cycle(B - 2, True, False)
            cycle(B - 1, False, False)
            for pair in range(TILES // 2):
                sp.wait_ge(out_stored[pair], 16 * (B + 1))

        @block.tensor
        def _(pe):
            def products(dst, terms, start=True, stop=True):
                for n, (lhs, rhs) in enumerate(terms):
                    last = nc.tensor.matmul(dst, lhs, rhs, start=start and n == 0,
                                            stop=stop and n == len(terms) - 1)
                return last

            def split_terms(l_hi, l_lo, r_hi, r_lo):
                return [(l_lo, r_hi), (l_hi, r_lo), (l_hi, r_hi)]

            def setup():
                pe.wait_ge(wqk_loaded, 32)
                for c in range(DC):
                    products(ps_acc[:, c, 0:D], [(wk_raw[:, f, c * P:(c + 1) * P], wq_raw[:, f, :])
                                                 for f in range(DC)]).then_inc(m_psum, 1)
                pe.wait_ge(small_loaded, 16 * 6)
                pe.wait_ge(bk_wide_set, DC)
                for c in range(DC):
                    products(ps_a[:, 2 * c:2 * c + 2], [(wq_raw[:, f, c * P:(c + 1) * P], bk_col[:, f, :])
                                                        for f in range(DC)])
                for c in range(DC):
                    products(ps_a[:, 4 + 2 * c:6 + 2 * c], [(wk_raw[:, f, c * P:(c + 1) * P], bq_col[:, f, :])
                                                            for f in range(DC)])
                products(ps_a[:, 8:10], [(bk_wide[:, f, :], bq_col[:, f, :]) for f in range(DC)]).then_inc(wb_psum, 1)
                pe.wait_ge(const_set, CONSTS)
                pe.wait_ge(abs_summed, 2)
                products(ps_b[:, 0:2], [(ones[:], abs_sum[:])]).then_inc(abs_psum, 1)

            def g_unit(b, u):
                half, c = u // DC, u % DC
                pe.wait_ge(xt_lo_set, NH * b + half + 1)
                if u:
                    pe.wait_ge(g_lo_set, NH * DC * b + u)
                else:
                    pe.wait_ge(m_lo_set, DC)
                    pe.wait_ge(bias_set, 3)
                cols = slice(half * HALF, (half + 1) * HALF)
                products(ps_a[:], [t for k in range(DC) for t in split_terms(
                    m_hi[:, k, c * P:(c + 1) * P], m_lo[:, k, c * P:(c + 1) * P],
                    xt_hi[:, k, cols], xt_lo[:, k, cols])]).then_inc(g_psum, 1)

            def v_and_scores(b, j, first):
                rows = slice(j * P, (j + 1) * P)
                if j >= 2:
                    pe.wait_ge(v_taken, TILES * b + j - 1)
                elif j == 0:
                    pe.wait_ge(g_lo_set, NH * DC * (b + 1))
                    pe.wait_ge(wv_lo_set, DC)
                    if first:
                        pe.wait_ge(scale_set, 1)
                    else:
                        pe.wait_ge(gelu_done, U * b)
                products(ps_v[j % 2][:, 0:DV], [t for k in range(DC) for t in split_terms(
                    xt_hi[:, k, rows], xt_lo[:, k, rows], wv_hi[:, k, :], wv_lo[:, k, :])]).then_inc(v_psum, 1)
                if j >= 2:
                    pe.wait_ge(exp_done, TILES * b + j - 1)
                for half in range(NH):
                    cols = slice(half * HALF, (half + 1) * HALF)
                    last = products(ps_s[:, j % 2, half, :], [t for k in range(DC) for t in split_terms(
                        g_hi[:, k, rows], g_lo[:, k, rows], xt_hi[:, k, cols], xt_lo[:, k, cols])])
                last.then_inc(s_psum, 1)

            def mix(b, i):
                rows = slice(i * P, (i + 1) * P)
                pe.wait_ge(acc_free, L * b + i + 1)
                for j in range(TILES):
                    if i == 0:
                        pe.wait_ge(p_lo_set, TILES * b + j + 1)
                        pe.wait_ge(v_lo_set, TILES * b + j + 1)
                    last = products(ps_acc[:, i % 2, 0:D], split_terms(
                        p_hi[:, j, rows], p_lo[:, j, rows], v_hi[:, j, :], v_lo[:, j, :]),
                        start=j == 0, stop=j == TILES - 1)
                last.then_inc(acc_psum, 1)

            def transpose_half(b, half):
                pe.wait_ge(normed, L * b + TPH * (half + 1))
                for c in range(DC):
                    for i in range(TPH):
                        last = nc.tensor.transpose(ps_s[:, 1, c, i * P:(i + 1) * P],
                                                   x1[:, half * TPH + i, c * P:(c + 1) * P], identity[:])
                    last.then_inc(t_psum, 1)

            def up(b, u):
                half, f = u // FC, u % FC
                if f == 0:
                    pe.wait_ge(t_lo_set, DC * (NH * b + half + 1))
                if u == 0:
                    pe.wait_ge(tern_set, 2)
                if u >= len(ps_h):
                    pe.wait_ge(gelu_done, U * b + u - len(ps_h) + 1)
                products(ps_h[u % len(ps_h)], [(w1[:, k, f * P:(f + 1) * P], part[:, k, :])
                                               for part in (x1t_lo, x1t_hi) for k in range(DC)]).then_inc(h_psum, 1)

            def down(b, t):
                half, cols = t // TPH, slice((t % TPH) * P, (t % TPH + 1) * P)
                pe.wait_ge(acc_free, L * b + TILES + t + 1)
                for f in range(FC):
                    if t % TPH == 0:
                        pe.wait_ge(h_lo_set, U * b + half * FC + f + 1)
                    last = products(ps_acc[:, t % 2, 0:D], [(h_lo[:, f, cols], w2[:, f, :]), (h_hi[:, f, cols], w2[:, f, :])],
                                    start=f == 0, stop=f == FC - 1)
                last.then_inc(acc_psum, 1)

            def attend(b, first=False):
                for j in range(TILES):
                    v_and_scores(b, j, first)
                    if not first and j in DOWN_AFTER:
                        for t in DOWN_AFTER[j]:
                            down(b - 1, t)

            def mix_and_feed(b, last=False):
                def g(u):
                    if not last:
                        g_unit(b + 1, u)
                mix(b, 0); mix(b, 1); mix(b, 2); g(0)
                mix(b, 3); g(1)
                mix(b, 4); transpose_half(b, 0); g(2)
                mix(b, 5); up(b, 0); up(b, 1)
                mix(b, 6); up(b, 2); up(b, 3); up(b, 4)
                mix(b, 7); g(3); up(b, 5); up(b, 6); up(b, 7)
                transpose_half(b, 1)
                for t in range(TPH):
                    down(b, t)
                for u in range(FC, U):
                    up(b, u)

            setup()
            for u in range(NH * DC):
                g_unit(0, u)
            attend(0, first=True)
            with pe.Fori(0, B - 1) as b:
                mix_and_feed(b)
                attend(b + 1)
            mix_and_feed(B - 1, last=True)
            for t in range(TPH, TILES):
                down(B - 1, t)

        @block.scalar
        def _(act):
            def setup():
                for c in range(DC):
                    act.wait_ge(m_psum, c + 1)
                    nc.scalar.activation(m_hi[:, c, :], ps_acc[:, c, 0:D], ACT.Copy).then_inc(m_hi_set, 1)
                act.wait_ge(wb_psum, 1)
                act.wait_ge(wv_loaded, 16)
                for c in range(DC):
                    nc.scalar.activation(wv_hi[:, c, 0:D], wv_raw[:, c, :], ACT.Copy)
                    nc.scalar.activation(wv_hi[:, c, D:DV], ps_a[:, 4 + 2 * c:6 + 2 * c], ACT.Copy).then_inc(wv_hi_set, 1)

            def xt_high(b, half, first=False):
                act.wait_ge(xt_loaded, 16 * (NH * b + half + 1))
                if not first:
                    act.wait_ge(s_psum, TILES * b)
                nc.scalar.activation(xt_hi[:, :, half * HALF:(half + 1) * HALF], xt_raw[:], ACT.Copy).then_inc(xt_hi_set, 1)

            def g_high(b, u):
                half, c = u // DC, u % DC
                act.wait_ge(g_psum, NH * DC * b + u + 1)
                nc.scalar.activation(g_hi[:, c, half * HALF:(half + 1) * HALF], ps_a[:], ACT.Identity,
                                     bias=g_bias[:, c:c + 1]).then_inc(g_hi_set, 1)

            def exponentials(b, j, first):
                act.wait_ge(bias_ready, TILES * b + j + 1)
                if j >= 2:
                    act.wait_ge(p_lo_set, TILES * b + j - 1)
                elif j == 0:
                    if first:
                        act.wait_ge(tern_set, 1)
                    else:
                        act.wait_ge(h_lo_set, U * b)
                nc.scalar.activation(p_f[:, j % 2, :], ps_s[:, j % 2, :, :], ACT.Exp, bias=s_bias[:, j:j + 1],
                                     scale=SCALE, accum_out=p_sum[:, j:j + 1]).then_inc(exp_done, 1)

            def p_high(b, j):
                act.wait_ge(exp_done, TILES * b + j + 1)
                nc.scalar.activation(p_hi[:, j, :], p_f[:, j % 2, :], ACT.Copy).then_inc(p_hi_set, 1)

            def v_high(b, j):
                act.wait_ge(rsum_set, TILES * b + j + 1)
                nc.scalar.activation(v_hi[:, j, :], v_f[:, j % 2, 0:D], ACT.Copy,
                                     scale=p_rsum[:, j:j + 1]).then_inc(v_hi_set, 1)

            def normalise(b, k):
                i = k % TILES
                act.wait_ge(shift_set, L * b + k + 1)
                nc.scalar.activation(x1[:, i, :], x1[:, i, :], ACT.Identity, bias=shift[:, k:k + 1],
                                     scale=rstd[:, k:k + 1]).then_inc(normed, 1)

            def t_high(b, half):
                for c in range(DC):
                    act.wait_ge(t_psum, DC * (NH * b + half) + c + 1)
                    if half:
                        act.wait_ge(h_psum, U * b + FC)
                    nc.scalar.activation(x1t_hi[:, c, :], ps_s[:, 1, c, :], ACT.Copy).then_inc(t_hi_set, 1)

            def gelu(b, u):
                f = u % FC
                act.wait_ge(h_psum, U * b + u + 1)
                if u >= RH:
                    act.wait_ge(h_lo_set, U * b + u - RH + 1)
                nc.scalar.activation(h_f[:, u % RH, :], ps_h[u % len(ps_h)], ACT.Gelu,
                                     bias=b1_col[:, f:f + 1]).then_inc(gelu_done, 1)
                if u % 2:
                    act.wait_ge(gelu_done, U * b + u + 1)
                    if u >= FC:
                        act.wait_ge(acc_psum, L * b + TILES + TPH)
                    nc.scalar.activation(h_hi[:, f, :], h_f[:, u % RH, :], ACT.Copy).then_inc(h_hi_act, 1)

            def attend(b, first=False):
                for j in range(TILES):
                    exponentials(b, j, first)
                    if j:
                        v_high(b, j - 1)
                    p_high(b, j)
                    if not first and j in NORM_AFTER:
                        for t in NORM_AFTER[j]:
                            normalise(b - 1, TILES + t)
                v_high(b, TILES - 1)
                if not first:
                    normalise(b - 1, L - 2)
                    normalise(b - 1, L - 1)

            def mix_and_feed(b, last=False):
                def g(u):
                    if not last:
                        g_high(b + 1, u)

                def n(k):
                    normalise(b, k)
                if not last:
                    xt_high(b + 1, 0)
                    xt_high(b + 1, 1)
                n(0); n(1); g(0); n(2); g(1); n(3)
                t_high(b, 0)
                g(2); n(4); gelu(b, 0); gelu(b, 1)
                n(5); gelu(b, 2); gelu(b, 3); gelu(b, 4)
                n(6); g(3); gelu(b, 5); gelu(b, 6); gelu(b, 7)
                n(7)
                t_high(b, 1)
                n(8); n(9); gelu(b, 8); n(10); gelu(b, 9); n(11)
                for u in range(FC + 2, U):
                    gelu(b, u)

            setup()
            xt_high(0, 0, first=True)
            xt_high(0, 1, first=True)
            for u in range(NH * DC):
                g_high(0, u)
            attend(0, first=True)
            with act.Fori(0, B - 1) as b:
                mix_and_feed(b)
                attend(b + 1)
            mix_and_feed(B - 1, last=True)
            for k in range(TILES + TPH, L):
                normalise(B - 1, k)

        @block.vector
        def _(dve):
            def setup():
                nc.vector.memset(ones[:], 1.0).then_inc(const_set, 1)
                nc.vector.memset(neg_half[:], -0.5).then_inc(const_set, 1)
                nc.vector.memset(eps[:], LN_EPS).then_inc(const_set, 1)
                nc.vector.memset(zero[:], 0.0).then_inc(const_set, 1)
                dve.wait_ge(const_set, CONSTS)
                dve.wait_ge(small_loaded, 16 * 6)
                for f in range(DC):
                    nc.vector.tensor_scalar(bk_wide[:, f, :], ones[:], bk_col[:, f, 0:1], None,
                                            ALU.mult).then_inc(bk_wide_set, 1)
                for c in range(DC):
                    dve.wait_ge(m_hi_set, c + 1)
                    nc.vector.tensor_tensor(m_lo[:, c, :], ps_acc[:, c, 0:D], m_hi[:, c, :].bitcast(F32),
                                            ALU.subtract).then_inc(m_lo_set, 1)
                dve.wait_ge(m_lo_set, DC)
                for q in range(TILES // 2):
                    nc.vector.tensor_copy(s_max[:, 2 + q:3 + q], ones[:, 0:1]).then_inc(out_stored[q], 16)
                nc.vector.tensor_copy(s_max[:, 0:2], ones[:, 0:2]).then_inc(acc_free, 2)
                dve.wait_ge(wv_hi_set, DC)
                for c in range(DC):
                    nc.vector.tensor_copy(g_bias[:, c:c + 1], ps_a[:, 2 * c:2 * c + 1]).then_inc(bias_set, 1)
                nc.vector.tensor_copy(v_bias[:, D:DV], ps_a[:, 8:10]).then_inc(bias_set, 1)
                for c in range(DC):
                    nc.vector.tensor_tensor(wv_lo[:, c, D:DV], ps_a[:, 4 + 2 * c:6 + 2 * c],
                                            wv_hi[:, c, D:DV].bitcast(F32), ALU.subtract)
                    nc.vector.tensor_tensor(wv_lo[:, c, 0:D], wv_raw[:, c, :], wv_hi[:, c, 0:D].bitcast(F32),
                                            ALU.subtract).then_inc(wv_lo_set, 1)
                raws = ((w1_raw, w1_loaded), (w2_raw, w2_loaded))
                for n, (raw, loaded) in enumerate(raws):
                    dve.wait_ge(loaded, 16)
                    flat = raw.rearrange("p a b -> p (a b)").rearrange("p (c k) -> p c k", c=32)
                    nc.vector.tensor_reduce(abs_part[:, n, :], flat, AX_X, ALU.add,
                                            apply_absolute_value=True).then_inc(abs_parts, 1)
                dve.wait_ge(abs_parts, 2)
                for n in range(2):
                    nc.vector.tensor_reduce(abs_sum[:, n:n + 1], abs_part[:, n, :], AX_X, ALU.add).then_inc(abs_summed, 1)
                dve.wait_ge(abs_psum, 1)
                nc.vector.tensor_scalar(abs_sum[:, :], ps_b[:, 0:2], 1.0 / (D * FF), MIN_SCALE,
                                        ALU.mult, ALU.max).then_inc(scale_set, 1)
                dve.wait_ge(scale_set, 1)
                for sign, factor in ((NEG, -0.5), (POS, 0.5)):
                    nc.vector.tensor_scalar(cut[:, :, sign], abs_sum[:, :], factor, None, ALU.mult).then_inc(cut_set, 1)
                dve.wait_ge(cut_set, 2)

            def ternary(n, raw, mask, dst):
                nc.vector.tensor_scalar(mask, raw, cut[:, n, NEG:NEG + 1], None, ALU.is_lt).then_inc(neg_set, 1)
                dve.wait_ge(neg_set, n + 1)
                nc.vector.scalar_tensor_tensor(dst, raw, cut[:, n, POS:POS + 1], mask.bitcast(F32),
                                               ALU.is_gt, ALU.subtract).then_inc(tern_set, 1)

            def flat(a):
                return a.rearrange("p a b -> p (a b)")

            def xt_low(b, half):
                dve.wait_ge(xt_hi_set, NH * b + half + 1)
                cols = slice(half * HALF, (half + 1) * HALF)
                nc.vector.tensor_tensor(xt_lo[:, :, cols], xt_raw[:], xt_hi[:, :, cols].bitcast(F32),
                                        ALU.subtract).then_inc(xt_lo_set, 1)

            def g_low(b, u):
                half, c = u // DC, u % DC
                cols = slice(half * HALF, (half + 1) * HALF)
                dve.wait_ge(g_hi_set, NH * DC * b + u + 1)
                nc.vector.scalar_tensor_tensor(g_lo[:, c, cols], ps_a[:], g_bias[:, c:c + 1],
                                               g_hi[:, c, cols].bitcast(F32), ALU.add, ALU.subtract).then_inc(g_lo_set, 1)

            def exp_bias(b, j):
                dve.wait_ge(v_psum, TILES * b + j + 1)
                dve.wait_ge(v_lo_set, TILES * b + max(j - 1, 0))
                nc.vector.tensor_tensor(v_f[:, j % 2, :], ps_v[j % 2][:, 0:DV], v_bias[:], ALU.add).then_inc(v_taken, 1)
                dve.wait_ge(s_psum, TILES * b + j + 1)
                nc.vector.tensor_reduce(s_max[:, j:j + 1], ps_s[:, j % 2, :, :].rearrange("p a n -> p (a n)"),
                                        AX_X, ALU.max).then_inc(max_set, 1)
                t = v_f[:, j % 2, D:D + 1]
                dve.wait_ge(v_taken, TILES * b + j + 1)
                dve.wait_ge(max_set, TILES * b + j + 1)
                nc.vector.tensor_scalar(s_top[:, j:j + 1], s_max[:, j:j + 1], t, None, ALU.add).then_inc(top_set, 1)
                dve.wait_ge(top_set, TILES * b + j + 1)
                nc.vector.tensor_scalar(s_bias[:, j:j + 1], t, s_top[:, j:j + 1], SCALE,
                                        ALU.subtract, ALU.mult).then_inc(bias_ready, 1)

            def p_and_v_low(b, j):
                dve.wait_ge(exp_done, TILES * b + j + 1)
                nc.vector.reciprocal(p_rsum[:, j:j + 1], p_sum[:, j:j + 1]).then_inc(rsum_set, 1)
                dve.wait_ge(p_hi_set, TILES * b + j + 1)
                nc.vector.tensor_tensor(p_lo[:, j, :], p_f[:, j % 2, :], p_hi[:, j, :].bitcast(F32),
                                        ALU.subtract).then_inc(p_lo_set, 1)
                dve.wait_ge(v_hi_set, TILES * b + j + 1)
                nc.vector.scalar_tensor_tensor(v_lo[:, j, :], v_f[:, j % 2, 0:D], p_rsum[:, j:j + 1],
                                               v_hi[:, j, :].bitcast(F32), ALU.mult, ALU.subtract).then_inc(v_lo_set, 1)

            def residual(b, k):
                i = k % TILES
                dve.wait_ge(acc_psum, L * b + k + 1)
                if k < TILES:
                    dve.wait_ge(x_loaded[(i // 2) % 2], 16 * (2 * b + i // 4 + 1))
                    if i % 2 == 0:
                        dve.wait_ge(out_stored[i // 2], 16 * (b + 1))
                    other = x_tok[:, i % 4, :]
                else:
                    if i % TPH == 0:
                        dve.wait_ge(b2_added, NH * b + i // TPH + 1)
                    other = x1[:, i, :]
                nc.vector.tensor_tensor(x1[:, i, :], ps_acc[:, i % 2, 0:D], other, ALU.add).then_inc(acc_free, 1)
                dve.wait_ge(acc_free, L * b + k + 3)
                nc.vector.bn_stats(stats[:, k, :], x1[:, i, :]).then_inc(stats_set, 1)
                dve.wait_ge(const_set, CONSTS)
                dve.wait_ge(stats_set, L * b + k + 1)
                nc.vector.bn_aggr(mean_var[:, k, :], stats[:, k, :]).then_inc(mv_set, 1)

            def t_low(b, half):
                for c in range(DC):
                    dve.wait_ge(t_hi_set, DC * (NH * b + half) + c + 1)
                    nc.vector.tensor_tensor(x1t_lo[:, c, :], ps_s[:, 1, c, :], x1t_hi[:, c, :].bitcast(F32),
                                            ALU.subtract).then_inc(t_lo_set, 1)

            def h_low(b, u):
                f = u % FC
                if u % 2:
                    dve.wait_ge(h_hi_act, U // 2 * b + u // 2 + 1)
                else:
                    dve.wait_ge(gelu_done, U * b + u + 1)
                    if u >= FC:
                        dve.wait_ge(acc_psum, L * b + TILES + TPH)
                    nc.vector.tensor_copy(h_hi[:, f, :], h_f[:, u % RH, :]).then_inc(h_hi_dve, 1)
                    dve.wait_ge(h_hi_dve, U // 2 * b + u // 2 + 1)
                nc.vector.tensor_tensor(h_lo[:, f, :], h_f[:, u % RH, :], h_hi[:, f, :].bitcast(F32),
                                        ALU.subtract).then_inc(h_lo_set, 1)

            def attend(b, first=False):
                for j in range(TILES):
                    exp_bias(b, j)
                    if j:
                        p_and_v_low(b, j - 1)
                    if not first and j in DOWN_AFTER and j < TILES - 1:
                        for t in DOWN_AFTER[j]:
                            residual(b - 1, TILES + t)
                p_and_v_low(b, TILES - 1)
                if not first:
                    for t in DOWN_AFTER[TILES - 1]:
                        residual(b - 1, TILES + t)

            def mix_and_feed(b, last=False):
                def g(u):
                    if not last:
                        g_low(b + 1, u)

                def r(k):
                    residual(b, k)
                if not last:
                    xt_low(b + 1, 0)
                    xt_low(b + 1, 1)
                r(0); r(1); r(2); g(0); r(3); g(1); r(4)
                t_low(b, 0)
                g(2); r(5); h_low(b, 0); h_low(b, 1)
                r(6); h_low(b, 2); h_low(b, 3); h_low(b, 4)
                r(7); g(3); h_low(b, 5); h_low(b, 6); h_low(b, 7)
                t_low(b, 1)
                r(8); r(9); r(10); r(11)
                for u in range(FC, U):
                    h_low(b, u)

            setup()
            ternary(0, flat(w1_raw), flat(p_hi[:, 0:2, :]), flat(w1[:]))
            xt_low(0, 0)
            xt_low(0, 1)
            for u in range(NH * DC):
                g_low(0, u)
            ternary(1, flat(w2_raw), flat(p_hi[:, 2:4, :]), flat(w2[:]))
            attend(0, first=True)
            with dve.Fori(0, B - 1) as b:
                mix_and_feed(b)
                attend(b + 1)
            mix_and_feed(B - 1, last=True)
            for t in range(TPH, TILES):
                residual(B - 1, TILES + t)

        @block.gpsimd
        def _(pool):
            def norm_factors(b, k):
                pool.wait_ge(mv_set, L * b + k + 1)
                nc.gpsimd.tensor_tensor(var_eps[:, k:k + 1], mean_var[:, k, 1:2], eps[:], ALU.add)
                nc.gpsimd.tensor_tensor(neg_mean[:, k:k + 1], zero[:], mean_var[:, k, 0:1], ALU.subtract).then_inc(eps_set, 1)
                pool.wait_ge(eps_set, L * b + k + 1)
                nc.gpsimd.tensor_tensor(rstd[:, k:k + 1], var_eps[:, k:k + 1], neg_half[:], ALU.pow).then_inc(rstd_set, 1)
                pool.wait_ge(rstd_set, L * b + k + 1)
                nc.gpsimd.tensor_tensor(shift[:, k:k + 1], neg_mean[:, k:k + 1], rstd[:, k:k + 1],
                                        ALU.mult).then_inc(shift_set, 1)

            def add_b2(b, half):
                pool.wait_ge(t_psum, DC * (NH * b + half + 1))
                tiles = x1[:, half * TPH:(half + 1) * TPH, :]
                nc.gpsimd.tensor_tensor(tiles, tiles, b2_row[:].unsqueeze(1).broadcast_to([P, TPH, D]),
                                        ALU.add).then_inc(b2_added, 1)

            def mix_and_feed(b):
                for k in range(5):
                    norm_factors(b, k)
                add_b2(b, 0)
                for k in range(5, 8):
                    norm_factors(b, k)
                add_b2(b, 1)
                for k in range(8, 12):
                    norm_factors(b, k)

            pool.wait_ge(const_set, CONSTS)
            pool.wait_ge(small_loaded, 16 * 6)
            with pool.Fori(0, B) as b:
                mix_and_feed(b)
                for k in range(12, L):
                    norm_factors(b, k)


DOWN_AFTER = {2: [4], 5: [5], 7: [6, 7]}
NORM_AFTER = {4: [4], 7: [5]}

_INS = ["x", "x_t", "w_qk", "w_v", "b_q", "b_k", "b_v", "w1_t", "b1", "w2_t", "b2", "eye"]


def kernel(L0_attn_x, L0_attn_W, L0_attn_b, L0_ffn_W1, L0_ffn_b1, L0_ffn_W2, L0_ffn_b2):
    import numpy as np
    import concourse.bacc as bacc
    from concourse import mybir as _mybir
    from concourse.bass_utils import run_bass_kernel_spmd as run

    x, W, b, W1, b1, W2, b2 = (np.asarray(a) for a in (
        L0_attn_x, L0_attn_W, L0_attn_b, L0_ffn_W1, L0_ffn_b1, L0_ffn_W2, L0_ffn_b2))
    B, S, D = x.shape
    FF = W1.shape[0]
    DC, FC, TILES, NH = D // P, FF // P, S // P, S // HALF

    def column(v):
        return np.stack([v.reshape(DC, P).T, np.zeros((P, DC), v.dtype)], axis=-1)

    arrays = {
        "x": x,
        "x_t": x.reshape(B, P, NH, TILES // NH, DC, P).transpose(0, 2, 5, 4, 3, 1).reshape(B, NH, P, DC, HALF),
        "w_qk": W[:2 * D].reshape(2, DC, P, D).transpose(2, 0, 1, 3),
        "w_v": W[2 * D:].T.reshape(DC, P, D).transpose(1, 0, 2),
        "b_q": column(b[:D]),
        "b_k": column(b[D:2 * D]),
        "b_v": b[2 * D:].reshape(1, D),
        "w1_t": W1.T.reshape(DC, P, FF).transpose(1, 0, 2),
        "b1": b1.reshape(FC, P).T,
        "w2_t": W2.T.reshape(FC, P, D).transpose(1, 0, 2),
        "b2": b2.reshape(1, D),
        "eye": np.eye(P, dtype=x.dtype),
    }
    arrays = {n: np.ascontiguousarray(a) for n, a in arrays.items()}
    nc = bacc.Bacc("TRN2", target_bir_lowering=False, num_devices=1)
    args = [nc.dram_tensor(f"in_{n}", arrays[n].shape, _mybir.dt.from_np(arrays[n].dtype),
                           kind="ExternalInput").ap() for n in _INS]
    out = nc.dram_tensor("out_0", x.shape, _mybir.dt.from_np(x.dtype), kind="ExternalOutput").ap()
    postln_block_kernel(nc, *args, out)
    r = run(nc, [{f"in_{n}": arrays[n] for n in _INS}], core_ids=[0])
    return r.results[0]["out_0"]
```

```python
from contextlib import ExitStack

import concourse.bass as bass
from concourse import mybir

ALU = mybir.AluOpType
ACT = mybir.ActivationFunctionType
F32 = mybir.dt.float32
F32R = mybir.dt.float32r
AX_X = mybir.AxisListType.X

P = 128
HALF = 512
LN_EPS = 1e-5
MIN_SCALE = 1e-8
W1, W2 = 0, 1


def postln_block_kernel(nc, x, x_t, w_qk, w_v, cols, rows, w1_t, w2_t, out):
    B, S, D = x.shape
    DC = D // P
    TILES = S // P
    NH = S // HALF
    TPH = HALF // P
    FF = w1_t.shape[2]
    FC = FF // P
    U = NH * FC
    DV = D + 2
    SCALE = 1.0 / D
    L = 2 * TILES
    assert D & (D - 1) == 0 and NH == 2 and DC == 2 and TILES == 8 and FC == 8

    with ExitStack() as ctx:
        def sb(name, shape, dt=F32):
            return ctx.enter_context(nc.sbuf_tensor(name, shape, dt))

        def ps(name, shape):
            return ctx.enter_context(nc.psum_tensor(name, shape, F32))

        def sem(name):
            return ctx.enter_context(nc.semaphore(name))

        ones = sb("ones", [P, P])
        column = sb("column", [P, 4 * DC + FC + P])
        row = sb("row", [P, 2, D])
        m_hi, m_lo = sb("m_hi", [P, DC, D], F32R), sb("m_lo", [P, DC, D], F32R)
        wv_hi, wv_lo = sb("wv_hi", [P, DC, DV], F32R), sb("wv_lo", [P, DC, DV], F32R)
        w1 = sb("w1", [P, DC, FF], F32R)
        w2 = sb("w2", [P, FC, D], F32R)
        g_bias = sb("g_bias", [P, DC])
        v_bias = sb("v_bias", [P, DV])
        bq_col = column[:, 0:2 * DC].rearrange("p (c z) -> p c z", z=2)
        bk_col = column[:, 2 * DC:4 * DC].rearrange("p (c z) -> p c z", z=2)
        b1_col = column[:, 4 * DC:4 * DC + FC]
        identity = column[:, 4 * DC + FC:]
        b2_row = row[:, 1, :]
        PARTS = 4
        abs_part = sb("abs_part", [P, 2, PARTS])
        abs_sum = sb("abs_sum", [P, 2])
        scale = sb("scale", [P, 2])
        cut = sb("cut", [P, 2])
        neg_half, eps, zero = sb("neg_half", [P, 1]), sb("eps", [P, 1]), sb("zero", [P, 1])
        CONSTS = 5
        xt_raw = sb("xt_raw", [P, DC, HALF])
        xt_hi, xt_lo = sb("xt_hi", [P, DC, S], F32R), sb("xt_lo", [P, DC, S], F32R)
        x_tok = sb("x_tok", [P, 4, D])
        g_hi, g_lo = sb("g_hi", [P, DC, S], F32R), sb("g_lo", [P, DC, S], F32R)
        v_f = sb("v_f", [P, 2, DV])
        v_hi, v_lo = sb("v_hi", [P, TILES, D], F32R), sb("v_lo", [P, TILES, D], F32R)
        p_f = sb("p_f", [P, 2, S])
        p_hi, p_lo = sb("p_hi", [P, TILES, S], F32R), sb("p_lo", [P, TILES, S], F32R)
        x1 = sb("x1", [P, TILES, D])
        x1t_hi, x1t_lo = sb("x1t_hi", [P, DC, HALF], F32R), sb("x1t_lo", [P, DC, HALF], F32R)
        h_hi, h_lo = sb("h_hi", [P, FC, HALF], F32R), sb("h_lo", [P, FC, HALF], F32R)
        s_max, s_top, s_bias = sb("s_max", [P, TILES]), sb("s_top", [P, TILES]), sb("s_bias", [P, TILES])
        p_sum, p_rsum = sb("p_sum", [P, TILES]), sb("p_rsum", [P, TILES])
        stats, mean_var = sb("stats", [P, L, 6]), sb("mean_var", [P, L, 2])
        var_eps, neg_mean = sb("var_eps", [P, L]), sb("neg_mean", [P, L])
        rstd, shift = sb("rstd", [P, L]), sb("shift", [P, L])
        h_f = p_f[:].rearrange("p a (c n) -> p (a c) n", n=HALF)
        RH = 4

        ps_s = ps("ps_s", [P, 2, 2, HALF])
        ps_acc = ps("ps_acc", [P, 2, HALF])
        ps_a = ps("ps_a", [P, HALF])
        ps_b = ps("ps_b", [P, HALF])
        ps_v = [ps_a, ps_b]
        def ps_g(u, first):
            return ps_s[:, u // DC, u % DC, :] if first else ps_a[:]

        ps_h = [ps_s[:, 0, 0, :], ps_s[:, 0, 1, :], ps_b[:]]

        wqk_loaded, wv_loaded = sem("wqk_loaded"), sem("wv_loaded")
        cols_loaded, rows_loaded = sem("cols_loaded"), sem("rows_loaded")
        tern_loaded = [sem("w1_loaded"), sem("w2_loaded")]
        xt1_loaded = sem("xt1_loaded")
        xt_loaded = sem("xt_loaded")
        x_loaded = [sem("x_loaded0"), sem("x_loaded1")]
        out_stored = [sem(f"out_stored{q}") for q in range(TILES // 2)]
        const_set = sem("const_set")
        bk_wide_set = sem("bk_wide_set")
        m_psum, wb_psum = sem("m_psum"), sem("wb_psum")
        m_hi_set, m_lo_set = sem("m_hi_set"), sem("m_lo_set")
        wv_hi_set, wv_lo_set, bias_set = sem("wv_hi_set"), sem("wv_lo_set"), sem("bias_set")
        sign_set, abs_set, abs_summed, abs_psum = sem("sign_set"), sem("abs_set"), sem("abs_summed"), sem("abs_psum")
        scale_set, cut_set, tern_set = sem("scale_set"), sem("cut_set"), sem("tern_set")
        xt_hi_set, xt_lo_set = sem("xt_hi_set"), sem("xt_lo_set")
        g_psum, g_hi_set, g_lo_set = sem("g_psum"), sem("g_hi_set"), sem("g_lo_set")
        v_psum, v_taken, v_hi_set, v_lo_set = sem("v_psum"), sem("v_taken"), sem("v_hi_set"), sem("v_lo_set")
        s_psum, max_set, top_set, bias_ready = sem("s_psum"), sem("max_set"), sem("top_set"), sem("bias_ready")
        exp_done, rsum_set = sem("exp_done"), sem("rsum_set")
        p_hi_set, p_lo_set = sem("p_hi_set"), sem("p_lo_set")
        acc_psum, acc_free = sem("acc_psum"), sem("acc_free")
        stats_set, mv_set = sem("stats_set"), sem("mv_set")
        eps_set, rstd_set, shift_set, normed = sem("eps_set"), sem("rstd_set"), sem("shift_set"), sem("normed")
        b2_added = sem("b2_added")
        t_psum, t_hi_set, t_lo_set = sem("t_psum"), sem("t_hi_set"), sem("t_lo_set")
        h_psum, gelu_done = sem("h_psum"), sem("gelu_done")
        h_hi_act, h_hi_dve, h_lo_set = sem("h_hi_act"), sem("h_hi_dve"), sem("h_lo_set")

        x_view = x.rearrange("b (p i) d -> b p i d", p=P)
        out_view = out.rearrange("b (p i) d -> b p i d", p=P)
        wq_raw, wk_raw, wv_raw = x1[:, 0:DC, :], x1[:, DC:2 * DC, :], x1[:, 2 * DC:3 * DC, :]
        tern_raw = [p_f[:].rearrange("p a b -> p (a b)"), x1[:].rearrange("p a b -> p (a b)")]
        tern_sign = [h_hi[:, n * FC // 2:(n + 1) * FC // 2, :].rearrange("p a b -> p (a b)") for n in (W1, W2)]
        tern_out = [w1[:].rearrange("p a b -> p (a b)"), w2[:].rearrange("p a b -> p (a b)")]
        xt_raw1 = x_tok[:].rearrange("p (c a) d -> p c (a d)", c=DC)
        bk_wide = v_f[:, :, 0:P]

        block = ctx.enter_context(nc.Block())

        @block.sync
        def _(sp):
            def wait_apart(semaphore, count):
                count = count if isinstance(count, int) else sp.to_reg(count)
                sp.wait_ge(wqk_loaded, 32)
                sp.wait_ge(semaphore, count)

            def load_xt(b, half):
                sp.dma_start(xt_raw[:], x_t[b, half]).then_inc(xt_loaded, 16)

            def load_x(b, pair):
                sp.dma_start(x_tok[:, 2 * (pair % 2):2 * (pair % 2) + 2, :],
                             x_view[b, :, 2 * pair:2 * pair + 2, :]).then_inc(x_loaded[pair % 2], 16)

            def cycle(b, next_xt, next2_xt):
                if next_xt:
                    wait_apart(xt_lo_set, 2 * b + 3)
                    load_xt(b + 1, 1)
                for pair in (2, 3):
                    wait_apart(acc_free, L * b + 2 * pair)
                    load_x(b, pair)
                if next2_xt:
                    wait_apart(xt_lo_set, 2 * b + 4)
                    load_xt(b + 2, 0)
                if next_xt:
                    for pair in (0, 1):
                        wait_apart(acc_free, L * b + 2 * pair + 8)
                        load_x(b + 1, pair)
                for pair in range(TILES // 2):
                    wait_apart(normed, L * b + TILES + 2 * pair + 2)
                    sp.dma_start(out_view[b, :, 2 * pair:2 * pair + 2, :],
                                 x1[:, 2 * pair:2 * pair + 2, :]).then_inc(out_stored[pair], 16)

            sp.dma_start(wq_raw, w_qk[:, 0]).then_inc(wqk_loaded, 16)
            sp.dma_start(wk_raw, w_qk[:, 1]).then_inc(wqk_loaded, 16)
            load_xt(0, 0)
            sp.dma_start(column[:], cols).then_inc(cols_loaded, 16)
            sp.dma_start(xt_raw1, x_t[0, 1]).then_inc(xt1_loaded, 16)
            sp.dma_start(wv_raw, w_v).then_inc(wv_loaded, 16)
            sp.dma_start(row[:], rows.rearrange("a (n d) -> a n d", n=2).broadcast_to([P, 2, D])).then_inc(rows_loaded, 16)
            sp.dma_start(p_f[:], w1_t).then_inc(tern_loaded[W1], 16)
            sp.wait_ge(wb_psum, 1)
            sp.wait_ge(wv_lo_set, DC)
            sp.dma_start(x1[:], w2_t).then_inc(tern_loaded[W2], 16)
            sp.wait_ge(xt_lo_set, 1)
            load_xt(1, 0)
            sp.wait_ge(xt_lo_set, 2)
            load_x(0, 0)
            load_x(0, 1)
            with sp.Fori(0, B - 2) as b:
                cycle(b, True, True)
            cycle(B - 2, True, False)
            cycle(B - 1, False, False)
            for pair in range(TILES // 2):
                sp.wait_ge(out_stored[pair], 16 * (B + 1))

        @block.tensor
        def _(pe):
            def products(dst, terms, start=True, stop=True):
                for n, (lhs, rhs) in enumerate(terms):
                    last = nc.tensor.matmul(dst, lhs, rhs, start=start and n == 0,
                                            stop=stop and n == len(terms) - 1)
                return last

            def split_terms(l_hi, l_lo, r_hi, r_lo):
                return [(l_lo, r_hi), (l_hi, r_lo), (l_hi, r_hi)]

            def setup():
                pe.wait_ge(wqk_loaded, 32)
                for c in range(DC):
                    products(ps_acc[:, c, 0:D], [(wk_raw[:, f, c * P:(c + 1) * P], wq_raw[:, f, :])
                                                 for f in range(DC)]).then_inc(m_psum, 1)
                pe.wait_ge(cols_loaded, 16)
                pe.wait_ge(bk_wide_set, DC)
                for c in range(DC):
                    products(ps_a[:, 2 * c:2 * c + 2], [(wq_raw[:, f, c * P:(c + 1) * P], bk_col[:, f, :])
                                                        for f in range(DC)])
                for c in range(DC):
                    products(ps_a[:, 4 + 2 * c:6 + 2 * c], [(wk_raw[:, f, c * P:(c + 1) * P], bq_col[:, f, :])
                                                            for f in range(DC)])
                products(ps_a[:, 8:10], [(bk_wide[:, f, :], bq_col[:, f, :]) for f in range(DC)]).then_inc(wb_psum, 1)

            def abs_total(n):
                pe.wait_ge(const_set, CONSTS)
                pe.wait_ge(acc_free, 2)
                pe.wait_ge(abs_summed, n + 1)
                products(ps_acc[:, n, 0:2], [(ones[:], abs_sum[:])]).then_inc(abs_psum, 1)

            def g_unit(b, u, first=False):
                half, c = u // DC, u % DC
                pe.wait_ge(xt_lo_set, NH * b + half + 1)
                if first:
                    pe.wait_ge(m_lo_set, DC)
                elif u:
                    pe.wait_ge(g_lo_set, NH * DC * b + u)
                cols = slice(half * HALF, (half + 1) * HALF)
                products(ps_g(u, first), [t for k in range(DC) for t in split_terms(
                    m_hi[:, k, c * P:(c + 1) * P], m_lo[:, k, c * P:(c + 1) * P],
                    xt_hi[:, k, cols], xt_lo[:, k, cols])]).then_inc(g_psum, 1)

            def v_and_scores(b, j, first):
                rows = slice(j * P, (j + 1) * P)
                if j >= 2:
                    pe.wait_ge(v_taken, TILES * b + j - 1)
                elif j == 0:
                    pe.wait_ge(g_lo_set, NH * DC * (b + 1))
                    pe.wait_ge(bias_set, 3)
                    pe.wait_ge(wv_lo_set, DC)
                elif not first:
                    pe.wait_ge(gelu_done, U * b)
                products(ps_v[j % 2][:, 0:DV], [t for k in range(DC) for t in split_terms(
                    xt_hi[:, k, rows], xt_lo[:, k, rows], wv_hi[:, k, :], wv_lo[:, k, :])]).then_inc(v_psum, 1)
                if j >= 2:
                    pe.wait_ge(exp_done, TILES * b + j - 1)
                for half in range(NH):
                    cols = slice(half * HALF, (half + 1) * HALF)
                    last = products(ps_s[:, (j + 1) % 2, half, :], [t for k in range(DC) for t in split_terms(
                        g_hi[:, k, rows], g_lo[:, k, rows], xt_hi[:, k, cols], xt_lo[:, k, cols])])
                last.then_inc(s_psum, 1)

            def mix(b, i):
                rows = slice(i * P, (i + 1) * P)
                pe.wait_ge(acc_free, L * b + i + 1)
                for j in range(TILES):
                    if i == 0:
                        pe.wait_ge(p_lo_set, TILES * b + j + 1)
                        pe.wait_ge(v_lo_set, TILES * b + j + 1)
                    last = products(ps_acc[:, i % 2, 0:D], split_terms(
                        p_hi[:, j, rows], p_lo[:, j, rows], v_hi[:, j, :], v_lo[:, j, :]),
                        start=j == 0, stop=j == TILES - 1)
                last.then_inc(acc_psum, 1)

            def transpose_half(b, half):
                pe.wait_ge(normed, L * b + TPH * (half + 1))
                for c in range(DC):
                    for i in range(TPH):
                        last = nc.tensor.transpose(ps_s[:, 1, c, i * P:(i + 1) * P],
                                                   x1[:, half * TPH + i, c * P:(c + 1) * P], identity[:])
                    last.then_inc(t_psum, 1)

            def up(b, u):
                half, f = u // FC, u % FC
                if f == 0:
                    pe.wait_ge(t_lo_set, DC * (NH * b + half + 1))
                if u == 0:
                    pe.wait_ge(tern_set, 2)
                if u >= len(ps_h):
                    pe.wait_ge(gelu_done, U * b + u - len(ps_h) + 1)
                products(ps_h[u % len(ps_h)], [(w1[:, k, f * P:(f + 1) * P], part[:, k, :])
                                               for part in (x1t_lo, x1t_hi) for k in range(DC)]).then_inc(h_psum, 1)

            def down(b, t):
                half, cols = t // TPH, slice((t % TPH) * P, (t % TPH + 1) * P)
                pe.wait_ge(acc_free, L * b + TILES + t + 1)
                for f in range(FC):
                    if t % TPH == 0:
                        pe.wait_ge(h_lo_set, U * b + half * FC + f + 1)
                    last = products(ps_acc[:, t % 2, 0:D], [(h_lo[:, f, cols], w2[:, f, :]), (h_hi[:, f, cols], w2[:, f, :])],
                                    start=f == 0, stop=f == FC - 1)
                last.then_inc(acc_psum, 1)

            def attend(b, first=False):
                for j in range(TILES):
                    v_and_scores(b, j, first)
                    if first and j == 2:
                        abs_total(W2)
                    if not first and j in DOWN_AFTER:
                        for t in DOWN_AFTER[j]:
                            down(b - 1, t)

            def mix_and_feed(b, last=False):
                def g(u):
                    if not last:
                        g_unit(b + 1, u)
                mix(b, 0); mix(b, 1); mix(b, 2); g(0)
                mix(b, 3); g(1)
                mix(b, 4); g(2); transpose_half(b, 0)
                mix(b, 5); up(b, 0); up(b, 1)
                mix(b, 6); up(b, 2); up(b, 3); up(b, 4)
                mix(b, 7); g(3); up(b, 5); up(b, 6); up(b, 7)
                transpose_half(b, 1)
                for t in range(TPH):
                    down(b, t)
                for u in range(FC, U):
                    up(b, u)

            setup()
            for u in range(NH * DC):
                g_unit(0, u, first=True)
            abs_total(W1)
            attend(0, first=True)
            with pe.Fori(0, B - 1) as b:
                mix_and_feed(b)
                attend(b + 1)
            mix_and_feed(B - 1, last=True)
            for t in range(TPH, TILES):
                down(B - 1, t)

        @block.scalar
        def _(act):
            def setup():
                for c in range(DC):
                    act.wait_ge(m_psum, c + 1)
                    nc.scalar.activation(m_hi[:, c, :], ps_acc[:, c, 0:D], ACT.Copy, scale=SCALE).then_inc(m_hi_set, 1)
                xt_high(0, 0, first=True)
                act.wait_ge(wb_psum, 1)
                act.wait_ge(wv_loaded, 16)
                for c in range(DC):
                    nc.scalar.activation(wv_hi[:, c, 0:D], wv_raw[:, c, :], ACT.Copy)
                    nc.scalar.activation(wv_hi[:, c, D:DV], ps_a[:, 4 + 2 * c:6 + 2 * c], ACT.Copy,
                                         scale=SCALE).then_inc(wv_hi_set, 1)
                xt_high(0, 1, first=True)

            def sign_and_sum(n):
                act.wait_ge(tern_loaded[n], 16)
                nc.scalar.activation(tern_sign[n], tern_raw[n], ACT.Sign).then_inc(sign_set, 1)
                act.wait_ge(sign_set, n + 1)
                size = D * FF // P // PARTS
                for k in range(PARTS):
                    part = tern_raw[n][:, k * size:(k + 1) * size]
                    nc.scalar.activation(part, part, ACT.Abs, accum_out=abs_part[:, n, k:k + 1]).then_inc(abs_set, 1)

            def xt_high(b, half, first=False):
                if first and half:
                    act.wait_ge(xt1_loaded, 16)
                else:
                    act.wait_ge(xt_loaded, 16 * (NH * b + half + first))
                if not first:
                    act.wait_ge(s_psum, TILES * b)
                raw = xt_raw1 if first and half else xt_raw[:]
                nc.scalar.activation(xt_hi[:, :, half * HALF:(half + 1) * HALF], raw, ACT.Copy).then_inc(xt_hi_set, 1)

            def g_high(b, u, first=False):
                half, c = u // DC, u % DC
                if first:
                    act.wait_ge(bias_set, DC)
                    act.wait_ge(rows_loaded, 16)
                act.wait_ge(g_psum, NH * DC * b + u + 1)
                nc.scalar.activation(g_hi[:, c, half * HALF:(half + 1) * HALF], ps_g(u, first), ACT.Identity,
                                     bias=g_bias[:, c:c + 1]).then_inc(g_hi_set, 1)

            def exponentials(b, j, first):
                act.wait_ge(bias_ready, TILES * b + j + 1)
                if j >= 2:
                    act.wait_ge(p_lo_set, TILES * b + j - 1)
                elif j == 0:
                    if first:
                        act.wait_ge(tern_set, 1)
                    else:
                        act.wait_ge(h_lo_set, U * b)
                nc.scalar.activation(p_f[:, j % 2, :], ps_s[:, (j + 1) % 2, :, :], ACT.Exp, bias=s_bias[:, j:j + 1],
                                     accum_out=p_sum[:, j:j + 1]).then_inc(exp_done, 1)

            def p_high(b, j):
                act.wait_ge(exp_done, TILES * b + j + 1)
                nc.scalar.activation(p_hi[:, j, :], p_f[:, j % 2, :], ACT.Copy).then_inc(p_hi_set, 1)

            def v_high(b, j):
                act.wait_ge(rsum_set, TILES * b + j + 1)
                nc.scalar.activation(v_hi[:, j, :], v_f[:, j % 2, 0:D], ACT.Copy,
                                     scale=p_rsum[:, j:j + 1]).then_inc(v_hi_set, 1)

            def normalise(b, k):
                i = k % TILES
                act.wait_ge(shift_set, L * b + k + 1)
                nc.scalar.activation(x1[:, i, :], x1[:, i, :], ACT.Identity, bias=shift[:, k:k + 1],
                                     scale=rstd[:, k:k + 1]).then_inc(normed, 1)

            def t_high(b, half):
                for c in range(DC):
                    act.wait_ge(t_psum, DC * (NH * b + half) + c + 1)
                    if half:
                        act.wait_ge(h_psum, U * b + FC)
                    nc.scalar.activation(x1t_hi[:, c, :], ps_s[:, 1, c, :], ACT.Copy).then_inc(t_hi_set, 1)

            def gelu(b, u):
                act.wait_ge(h_psum, U * b + u + 1)
                if u >= RH:
                    act.wait_ge(h_lo_set, U * b + u - RH + 1)
                nc.scalar.activation(h_f[:, u % RH, :], ps_h[u % len(ps_h)], ACT.Gelu,
                                     bias=b1_col[:, u % FC:u % FC + 1]).then_inc(gelu_done, 1)

            def h_high(b, u):
                act.wait_ge(gelu_done, U * b + u + 1)
                if u >= FC:
                    act.wait_ge(acc_psum, L * b + TILES + TPH)
                nc.scalar.activation(h_hi[:, u % FC, :], h_f[:, u % RH, :], ACT.Copy).then_inc(h_hi_act, 1)

            def gelus(b, units):
                for u in units:
                    gelu(b, u)
                    if u - 1 in H_HIGH_ACT:
                        h_high(b, u - 1)

            def attend(b, first=False):
                for j in range(TILES):
                    exponentials(b, j, first)
                    p_high(b, j)
                    v_high(b, j)
                    if first and j == 0:
                        sign_and_sum(W2)
                    if not first:
                        for k in {0: [8, 9], 1: [10, 11], 6: [12]}.get(j, []):
                            normalise(b - 1, k)
                if not first:
                    for k in range(L - 3, L):
                        normalise(b - 1, k)

            def mix_and_feed(b, last=False):
                def g(u):
                    if not last:
                        g_high(b + 1, u)

                def n(k):
                    normalise(b, k)
                def x_half(half):
                    if not last:
                        xt_high(b + 1, half)
                x_half(0); n(0); n(1); x_half(1); g(0); n(2); g(1); n(3); g(2)
                t_high(b, 0)
                n(4); gelus(b, [0, 1]); n(5); gelus(b, [2, 3, 4]); n(6)
                g(3); gelus(b, [5]); n(7); gelus(b, [6, 7])
                t_high(b, 1)
                gelus(b, range(FC, U))

            setup()
            sign_and_sum(W1)
            for u in range(NH * DC):
                g_high(0, u, first=True)
            attend(0, first=True)
            with act.Fori(0, B - 1) as b:
                mix_and_feed(b)
                attend(b + 1)
            mix_and_feed(B - 1, last=True)
            for k in range(TILES, L):
                normalise(B - 1, k)

        @block.vector
        def _(dve):
            def setup():
                nc.vector.memset(ones[:], 1.0).then_inc(const_set, 1)
                nc.vector.memset(neg_half[:], -0.5).then_inc(const_set, 1)
                nc.vector.memset(eps[:], LN_EPS).then_inc(const_set, 1)
                nc.vector.memset(zero[:], 0.0).then_inc(const_set, 1)
                nc.vector.memset(abs_sum[:], 0.0).then_inc(const_set, 1)
                dve.wait_ge(const_set, CONSTS)
                for q in range(TILES // 2):
                    nc.vector.tensor_copy(s_max[:, 2 + q:3 + q], ones[:, 0:1]).then_inc(out_stored[q], 16)
                xt_low(0, 0, first=True)
                dve.wait_ge(cols_loaded, 16)
                for f in range(DC):
                    nc.vector.tensor_scalar(bk_wide[:, f, :], ones[:], bk_col[:, f, 0:1], None,
                                            ALU.mult).then_inc(bk_wide_set, 1)
                for c in range(DC):
                    dve.wait_ge(m_hi_set, c + 1)
                    nc.vector.scalar_tensor_tensor(m_lo[:, c, :], ps_acc[:, c, 0:D], SCALE, m_hi[:, c, :].bitcast(F32),
                                                   ALU.mult, ALU.subtract).then_inc(m_lo_set, 1)
                dve.wait_ge(m_lo_set, DC)
                nc.vector.tensor_copy(s_max[:, 0:2], ones[:, 0:2]).then_inc(acc_free, 2)
                dve.wait_ge(wv_hi_set, DC)
                for c in range(DC):
                    nc.vector.tensor_scalar(g_bias[:, c:c + 1], ps_a[:, 2 * c:2 * c + 1], SCALE, None,
                                            ALU.mult).then_inc(bias_set, 1)
                dve.wait_ge(rows_loaded, 16)
                nc.vector.tensor_copy(v_bias[:, 0:D], row[:, 0, :])
                nc.vector.tensor_scalar(v_bias[:, D:DV], ps_a[:, 8:10], SCALE, None, ALU.mult).then_inc(bias_set, 1)
                for c in range(DC):
                    nc.vector.scalar_tensor_tensor(wv_lo[:, c, D:DV], ps_a[:, 4 + 2 * c:6 + 2 * c], SCALE,
                                                   wv_hi[:, c, D:DV].bitcast(F32), ALU.mult, ALU.subtract)
                    nc.vector.tensor_tensor(wv_lo[:, c, 0:D], wv_raw[:, c, :], wv_hi[:, c, 0:D].bitcast(F32),
                                            ALU.subtract).then_inc(wv_lo_set, 1)
                xt_low(0, 1, first=True)

            def abs_sums(n):
                dve.wait_ge(abs_set, PARTS * (n + 1))
                nc.vector.tensor_reduce(abs_sum[:, n:n + 1], abs_part[:, n, :], AX_X, ALU.add).then_inc(abs_summed, 1)

            def ternary(n):
                dve.wait_ge(abs_psum, n + 1)
                nc.vector.tensor_scalar(scale[:, n:n + 1], ps_acc[:, n, n:n + 1], 1.0 / (D * FF), MIN_SCALE,
                                        ALU.mult, ALU.max).then_inc(scale_set, 1)
                dve.wait_ge(scale_set, n + 1)
                nc.vector.tensor_scalar(cut[:, n:n + 1], scale[:, n:n + 1], 0.5, None, ALU.mult).then_inc(cut_set, 1)
                dve.wait_ge(cut_set, n + 1)
                nc.vector.scalar_tensor_tensor(tern_out[n], tern_raw[n], cut[:, n:n + 1], tern_sign[n].bitcast(F32),
                                               ALU.is_gt, ALU.mult).then_inc(tern_set, 1)

            def xt_low(b, half, first=False):
                dve.wait_ge(xt_hi_set, NH * b + half + 1)
                cols = slice(half * HALF, (half + 1) * HALF)
                raw = xt_raw1 if first and half else xt_raw[:]
                nc.vector.tensor_tensor(xt_lo[:, :, cols], raw, xt_hi[:, :, cols].bitcast(F32),
                                        ALU.subtract).then_inc(xt_lo_set, 1)

            def g_low(b, u, first=False):
                half, c = u // DC, u % DC
                cols = slice(half * HALF, (half + 1) * HALF)
                dve.wait_ge(g_hi_set, NH * DC * b + u + 1)
                nc.vector.scalar_tensor_tensor(g_lo[:, c, cols], ps_g(u, first), g_bias[:, c:c + 1],
                                               g_hi[:, c, cols].bitcast(F32), ALU.add, ALU.subtract).then_inc(g_lo_set, 1)

            def softmax_sums(b, j):
                dve.wait_ge(exp_done, TILES * b + j + 1)
                nc.vector.reciprocal(p_rsum[:, j:j + 1], p_sum[:, j:j + 1]).then_inc(rsum_set, 1)

            def v_and_max(b, j):
                dve.wait_ge(v_psum, TILES * b + j + 1)
                dve.wait_ge(v_lo_set, TILES * b + max(j - 1, 0))
                nc.vector.tensor_tensor(v_f[:, j % 2, :], ps_v[j % 2][:, 0:DV], v_bias[:], ALU.add).then_inc(v_taken, 1)
                dve.wait_ge(s_psum, TILES * b + j + 1)
                nc.vector.tensor_reduce(s_max[:, j:j + 1], ps_s[:, (j + 1) % 2, :, :].rearrange("p a n -> p (a n)"),
                                        AX_X, ALU.max, negate=True).then_inc(max_set, 1)

            def exp_bias(b, j):
                t = v_f[:, j % 2, D:D + 1]
                dve.wait_ge(v_taken, TILES * b + j + 1)
                dve.wait_ge(max_set, TILES * b + j + 1)
                nc.vector.scalar_tensor_tensor(s_bias[:, j:j + 1], s_max[:, j:j + 1], t, t,
                                               ALU.subtract, ALU.add).then_inc(bias_ready, 1)

            def p_low(b, j):
                dve.wait_ge(p_hi_set, TILES * b + j + 1)
                nc.vector.tensor_tensor(p_lo[:, j, :], p_f[:, j % 2, :], p_hi[:, j, :].bitcast(F32),
                                        ALU.subtract).then_inc(p_lo_set, 1)

            def v_low(b, j):
                dve.wait_ge(rsum_set, TILES * b + j + 1)
                dve.wait_ge(v_hi_set, TILES * b + j + 1)
                nc.vector.scalar_tensor_tensor(v_lo[:, j, :], v_f[:, j % 2, 0:D], p_rsum[:, j:j + 1],
                                               v_hi[:, j, :].bitcast(F32), ALU.mult, ALU.subtract).then_inc(v_lo_set, 1)

            def residual(b, k):
                i = k % TILES
                dve.wait_ge(acc_psum, L * b + k + 1)
                if k < TILES:
                    dve.wait_ge(x_loaded[(i // 2) % 2], 16 * (2 * b + i // 4 + 1))
                    if i % 2 == 0:
                        dve.wait_ge(out_stored[i // 2], 16 * (b + 1))
                    other = x_tok[:, i % 4, :]
                else:
                    if i % TPH == 0:
                        dve.wait_ge(b2_added, NH * b + i // TPH + 1)
                    other = x1[:, i, :]
                nc.vector.tensor_tensor(x1[:, i, :], ps_acc[:, i % 2, 0:D], other, ALU.add).then_inc(acc_free, 1)
                dve.wait_ge(acc_free, L * b + k + 3)
                nc.vector.bn_stats(stats[:, k, :], x1[:, i, :]).then_inc(stats_set, 1)
                dve.wait_ge(const_set, CONSTS)
                dve.wait_ge(stats_set, L * b + k + 1)
                nc.vector.bn_aggr(mean_var[:, k, :], stats[:, k, :]).then_inc(mv_set, 1)

            def t_low(b, half):
                for c in range(DC):
                    dve.wait_ge(t_hi_set, DC * (NH * b + half) + c + 1)
                    nc.vector.tensor_tensor(x1t_lo[:, c, :], ps_s[:, 1, c, :], x1t_hi[:, c, :].bitcast(F32),
                                            ALU.subtract).then_inc(t_lo_set, 1)

            def h_high(b, u):
                dve.wait_ge(gelu_done, U * b + u + 1)
                if u >= FC:
                    dve.wait_ge(acc_psum, L * b + TILES + TPH)
                nc.vector.tensor_copy(h_hi[:, u % FC, :], h_f[:, u % RH, :]).then_inc(h_hi_dve, 1)

            def h_low(b, u):
                f = u % FC
                if u in H_HIGH_ACT:
                    dve.wait_ge(h_hi_act, len(H_HIGH_ACT) * b + len([n for n in H_HIGH_ACT if n <= u]))
                else:
                    dve.wait_ge(h_hi_dve, (U - len(H_HIGH_ACT)) * b + len([n for n in range(u + 1) if n not in H_HIGH_ACT]))
                nc.vector.tensor_tensor(h_lo[:, f, :], h_f[:, u % RH, :], h_hi[:, f, :].bitcast(F32),
                                        ALU.subtract).then_inc(h_lo_set, 1)

            def h_halves(b, units):
                for n, u in enumerate(units):
                    if u not in H_HIGH_ACT:
                        h_high(b, u)
                    if n:
                        h_low(b, u - 1)
                h_low(b, units[-1])

            def attend(b, first=False):
                for j in range(TILES):
                    if j:
                        softmax_sums(b, j - 1)
                    v_and_max(b, j)
                    if j:
                        v_low(b, j - 1)
                    exp_bias(b, j)
                    if not first and j == TILES - 1:
                        residual(b - 1, L - 3)
                    if j:
                        p_low(b, j - 1)
                    if first and j == 1:
                        abs_sums(W2)
                    if first and j == 3:
                        ternary(W2)
                    if not first and j in DOWN_AFTER and j < TILES - 1:
                        for t in DOWN_AFTER[j]:
                            residual(b - 1, TILES + t)
                softmax_sums(b, TILES - 1)
                p_low(b, TILES - 1)
                v_low(b, TILES - 1)
                if not first:
                    residual(b - 1, L - 2)
                    residual(b - 1, L - 1)

            def mix_and_feed(b, last=False):
                def g(u):
                    if not last:
                        g_low(b + 1, u)

                def r(k):
                    residual(b, k)
                def x_half(half):
                    if not last:
                        xt_low(b + 1, half)
                r(0); x_half(0); r(1); r(2); g(0); x_half(1); r(3); g(1); r(4); g(2)
                t_low(b, 0)
                r(5); h_halves(b, range(0, 2)); r(6); h_halves(b, range(2, 5))
                r(7); g(3); h_halves(b, range(5, 8))
                t_low(b, 1)
                r(8); r(9); r(10); r(11)
                h_halves(b, range(FC, U))

            setup()
            abs_sums(W1)
            for u in range(NH * DC):
                g_low(0, u, first=True)
            ternary(W1)
            attend(0, first=True)
            with dve.Fori(0, B - 1) as b:
                mix_and_feed(b)
                attend(b + 1)
            mix_and_feed(B - 1, last=True)
            for t in range(TPH, TILES):
                residual(B - 1, TILES + t)

        @block.gpsimd
        def _(pool):
            def norm_factors(b, k):
                pool.wait_ge(mv_set, L * b + k + 1)
                nc.gpsimd.tensor_tensor(var_eps[:, k:k + 1], mean_var[:, k, 1:2], eps[:], ALU.add)
                nc.gpsimd.tensor_tensor(neg_mean[:, k:k + 1], zero[:], mean_var[:, k, 0:1], ALU.subtract).then_inc(eps_set, 1)
                pool.wait_ge(eps_set, L * b + k + 1)
                nc.gpsimd.tensor_tensor(rstd[:, k:k + 1], var_eps[:, k:k + 1], neg_half[:], ALU.pow).then_inc(rstd_set, 1)
                pool.wait_ge(rstd_set, L * b + k + 1)
                nc.gpsimd.tensor_tensor(shift[:, k:k + 1], neg_mean[:, k:k + 1], rstd[:, k:k + 1],
                                        ALU.mult).then_inc(shift_set, 1)

            def add_b2(b, half):
                pool.wait_ge(t_psum, DC * (NH * b + half + 1))
                tiles = x1[:, half * TPH:(half + 1) * TPH, :]
                nc.gpsimd.tensor_tensor(tiles, tiles, b2_row[:].unsqueeze(1).broadcast_to([P, TPH, D]),
                                        ALU.add).then_inc(b2_added, 1)

            def mix_and_feed(b):
                for k in range(5):
                    norm_factors(b, k)
                add_b2(b, 0)
                for k in range(5, 8):
                    norm_factors(b, k)
                add_b2(b, 1)
                for k in range(8, 12):
                    norm_factors(b, k)

            pool.wait_ge(const_set, CONSTS)
            pool.wait_ge(rows_loaded, 16)
            with pool.Fori(0, B) as b:
                mix_and_feed(b)
                for k in range(12, L):
                    norm_factors(b, k)


DOWN_AFTER = {3: [4], 7: [5, 6, 7]}
H_HIGH_ACT = [3, 6, 9, 11, 13]

_INS = ["x", "x_t", "w_qk", "w_v", "cols", "rows", "w1_t", "w2_t"]


def kernel(L0_attn_x, L0_attn_W, L0_attn_b, L0_ffn_W1, L0_ffn_b1, L0_ffn_W2, L0_ffn_b2):
    import numpy as np
    import concourse.bacc as bacc
    from concourse import mybir as _mybir
    from concourse.bass_utils import run_bass_kernel_spmd as run

    x, W, b, W1, b1, W2, b2 = (np.asarray(a) for a in (
        L0_attn_x, L0_attn_W, L0_attn_b, L0_ffn_W1, L0_ffn_b1, L0_ffn_W2, L0_ffn_b2))
    B, S, D = x.shape
    FF = W1.shape[0]
    DC, FC, TILES, NH = D // P, FF // P, S // P, S // HALF

    def column(v):
        return np.stack([v.reshape(DC, P).T, np.zeros((P, DC), v.dtype)], axis=-1).reshape(P, 2 * DC)

    arrays = {
        "x": x,
        "x_t": x.reshape(B, P, NH, TILES // NH, DC, P).transpose(0, 2, 5, 4, 3, 1).reshape(B, NH, P, DC, HALF),
        "w_qk": W[:2 * D].reshape(2, DC, P, D).transpose(2, 0, 1, 3),
        "w_v": W[2 * D:].T.reshape(DC, P, D).transpose(1, 0, 2),
        "cols": np.concatenate([column(b[:D]), column(b[D:2 * D]), b1.reshape(FC, P).T,
                                np.eye(P, dtype=x.dtype)], axis=1),
        "rows": np.concatenate([b[2 * D:], b2]).reshape(1, 2 * D),
        "w1_t": W1.T.reshape(DC, P, FF).transpose(1, 0, 2),
        "w2_t": W2.T.reshape(FC, P, D).transpose(1, 0, 2),
    }
    arrays = {n: np.ascontiguousarray(a) for n, a in arrays.items()}
    nc = bacc.Bacc("TRN2", target_bir_lowering=False, num_devices=1)
    args = [nc.dram_tensor(f"in_{n}", arrays[n].shape, _mybir.dt.from_np(arrays[n].dtype),
                           kind="ExternalInput").ap() for n in _INS]
    out = nc.dram_tensor("out_0", x.shape, _mybir.dt.from_np(x.dtype), kind="ExternalOutput").ap()
    postln_block_kernel(nc, *args, out)
    r = run(nc, [{f"in_{n}": arrays[n] for n in _INS}], core_ids=[0])
    return r.results[0]["out_0"]
```

```python
from contextlib import ExitStack

import concourse.bass as bass
from concourse import mybir

ALU = mybir.AluOpType
ACT = mybir.ActivationFunctionType
F32 = mybir.dt.float32
F32R = mybir.dt.float32r
AX_X = mybir.AxisListType.X

P = 128
HALF = 512
LN_EPS = 1e-5
MIN_SCALE = 1e-8
W1, W2 = 0, 1

WARM_UP = 8
W2_SUMS_AFTER = {1: [0], 2: [1], 3: [2, 3]}
DOWN_AFTER = {3: [4], 7: [5, 6, 7]}
UP_EARLY = 4
H_HIGH_ACT = [3, 6, 9, 11, 13, 15]


def postln_block_kernel(nc, x, x_t, w_qk, w_v, cols, rows, w1_t, w2_t, out):
    B, S, D = x.shape
    DC = D // P
    TILES = S // P
    NH = S // HALF
    TPH = HALF // P
    FF = w1_t.shape[2]
    FC = FF // P
    U = NH * FC
    DV = D + 2
    SCALE = 1.0 / D
    L = 2 * TILES
    assert D & (D - 1) == 0 and NH == 2 and DC == 2 and TILES == 8 and FC == 8

    with ExitStack() as ctx:
        def sb(name, shape, dt=F32):
            return ctx.enter_context(nc.sbuf_tensor(name, shape, dt))

        def ps(name, shape):
            return ctx.enter_context(nc.psum_tensor(name, shape, F32))

        def sem(name):
            return ctx.enter_context(nc.semaphore(name))

        ones = sb("ones", [P, P])
        bqk = sb("bqk", [P, DC, 2])
        column = sb("column", [P, 4 * DC + FC + P])
        b2_row = sb("b2_row", [P, D])
        m_hi, m_lo = sb("m_hi", [P, DC, D], F32R), sb("m_lo", [P, DC, D], F32R)
        wv_hi, wv_lo = sb("wv_hi", [P, DC, DV], F32R), sb("wv_lo", [P, DC, DV], F32R)
        w1 = sb("w1", [P, DC, FF], F32R)
        w2 = sb("w2", [P, FC, D], F32R)
        g_bias = sb("g_bias", [P, DC])
        v_bias = sb("v_bias", [P, DV])
        bq_col = column[:, 0:2 * DC].rearrange("p (c z) -> p c z", z=2)
        bk_col = column[:, 2 * DC:4 * DC].rearrange("p (c z) -> p c z", z=2)
        b1_col = column[:, 4 * DC:4 * DC + FC]
        identity = column[:, 4 * DC + FC:]
        PARTS = 4
        TERN_PARTS = [2, 4]
        abs_part = sb("abs_part", [P, 2, PARTS])
        abs_sum = sb("abs_sum", [P, 2, 2])
        scale = sb("scale", [P, 2])
        cut = sb("cut", [P, 2])
        neg_half, eps, zero = sb("neg_half", [P, 1]), sb("eps", [P, 1]), sb("zero", [P, 1])
        CONSTS = 5
        xt_raw = sb("xt_raw", [P, DC, HALF])
        xt_hi, xt_lo = sb("xt_hi", [P, DC, S], F32R), sb("xt_lo", [P, DC, S], F32R)
        x_tok = sb("x_tok", [P, 4, D])
        g_hi, g_lo = sb("g_hi", [P, DC, S], F32R), sb("g_lo", [P, DC, S], F32R)
        v_f, v_scaled = sb("v_f", [P, 2, DV]), sb("v_scaled", [P, D])
        v_hl = sb("v_hl", [P, TILES, 2, D], F32R)
        p_f = sb("p_f", [P, 2, S])
        p_hi, p_lo = sb("p_hi", [P, TILES, S], F32R), sb("p_lo", [P, TILES, S], F32R)
        x1 = sb("x1", [P, TILES, D])
        x1t_hi, x1t_lo = sb("x1t_hi", [P, DC, HALF], F32R), sb("x1t_lo", [P, DC, HALF], F32R)
        h_hi, h_lo = sb("h_hi", [P, FC, HALF], F32R), sb("h_lo", [P, FC, HALF], F32R)
        s_max, s_bias = sb("s_max", [P, TILES]), sb("s_bias", [P, TILES])
        p_sum, p_rsum = sb("p_sum", [P, TILES]), sb("p_rsum", [P, TILES])
        stats, mean_var = sb("stats", [P, L, 6]), sb("mean_var", [P, L, 2])
        var_eps, neg_mean = sb("var_eps", [P, L]), sb("neg_mean", [P, L])
        rstd, shift = sb("rstd", [P, L]), sb("shift", [P, L])
        h_f = p_f[:].rearrange("p a (c n) -> p (a c) n", n=HALF)
        RH = 4

        ps_s = ps("ps_s", [P, 2, 2, HALF])
        ps_acc = ps("ps_acc", [P, 2, HALF])
        ps_a = ps("ps_a", [P, HALF])
        ps_b = ps("ps_b", [P, HALF])
        ps_v = [ps_a, ps_b]

        def ps_g(u, first):
            return ps_s[:, 1 - u // DC, u % DC, :] if first else ps_a[:]

        ps_h = [ps_s[:, 0, 0, :], ps_s[:, 0, 1, :], ps_b[:]]

        wqk_loaded, wv_loaded = sem("wqk_loaded"), sem("wv_loaded")
        cols_loaded, rows_loaded = sem("cols_loaded"), sem("rows_loaded")
        tern_loaded = [sem("w1_loaded"), sem("w2_loaded")]
        xt0_loaded = sem("xt0_loaded")
        xt1_loaded = sem("xt1_loaded")
        xt_loaded = sem("xt_loaded")
        x_loaded = [sem("x_loaded0"), sem("x_loaded1")]
        out_stored = [sem(f"out_stored{q}") for q in range(TILES // 2)]
        const_set = sem("const_set")
        bqk_set, wb_hi_set = sem("bqk_set"), sem("wb_hi_set")
        m_psum, wb_psum = sem("m_psum"), sem("wb_psum")
        m_hi_set, m_lo_set = sem("m_hi_set"), sem("m_lo_set")
        wv_hi_set, wv_lo_set, bias_set = sem("wv_hi_set"), sem("wv_lo_set"), sem("bias_set")
        sign_set, abs_set, abs_summed, abs_psum = sem("sign_set"), sem("abs_set"), sem("abs_summed"), sem("abs_psum")
        scale_set, cut_set, tern_set = sem("scale_set"), sem("cut_set"), sem("tern_set")
        xt_hi_set, xt_lo_set = sem("xt_hi_set"), sem("xt_lo_set")
        g_psum, g_hi_set, g_lo_set = sem("g_psum"), sem("g_hi_set"), sem("g_lo_set")
        v_scaled_set = sem("v_scaled_set")
        v_psum, v_taken, v_hi_set, v_lo_set = sem("v_psum"), sem("v_taken"), sem("v_hi_set"), sem("v_lo_set")
        s_psum, max_set, bias_ready = sem("s_psum"), sem("max_set"), sem("bias_ready")
        exp_done, rsum_set = sem("exp_done"), sem("rsum_set")
        p_hi_set, p_lo_set = sem("p_hi_set"), sem("p_lo_set")
        low_added = sem("low_added")
        acc_psum, acc_free = sem("acc_psum"), sem("acc_free")
        stats_set, mv_set = sem("stats_set"), sem("mv_set")
        eps_set, rstd_set, shift_set, normed = sem("eps_set"), sem("rstd_set"), sem("shift_set"), sem("normed")
        b2_added = sem("b2_added")
        t_psum, t_hi_set, t_lo_set = sem("t_psum"), sem("t_hi_set"), sem("t_lo_set")
        h_psum, gelu_done = sem("h_psum"), sem("gelu_done")
        h_hi_act, h_hi_dve, h_lo_set = sem("h_hi_act"), sem("h_hi_dve"), sem("h_lo_set")

        x_view = x.rearrange("b (p i) d -> b p i d", p=P)
        out_view = out.rearrange("b (p i) d -> b p i d", p=P)
        wq_raw, wk_raw, wv_raw = x1[:, 0:DC, :], x1[:, DC:2 * DC, :], x1[:, 2 * DC:3 * DC, :]
        tern_raw = [p_f[:].rearrange("p a b -> p (a b)"), x1[:].rearrange("p a b -> p (a b)")]
        tern_sign = [h_hi[:, n * FC // 2:(n + 1) * FC // 2, :].rearrange("p a b -> p (a b)") for n in (W1, W2)]
        tern_out = [w1[:].rearrange("p a b -> p (a b)"), w2[:].rearrange("p a b -> p (a b)")]
        xt_raw1 = x_tok[:].rearrange("p (c a) d -> p c (a d)", c=DC)

        block = ctx.enter_context(nc.Block())

        @block.sync
        def _(sp):
            def wait_apart(semaphore, count):
                count = count if isinstance(count, int) else sp.to_reg(count)
                sp.wait_ge(wqk_loaded, 32)
                sp.wait_ge(semaphore, count)

            def load_xt(b, half):
                sp.dma_start(xt_raw[:], x_t[b, half]).then_inc(xt_loaded, 16)

            def load_x(b, pair):
                sp.dma_start(x_tok[:, 2 * (pair % 2):2 * (pair % 2) + 2, :],
                             x_view[b, :, 2 * pair:2 * pair + 2, :]).then_inc(x_loaded[pair % 2], 16)

            def cycle(b, next_xt, next2_xt):
                if next_xt:
                    wait_apart(xt_lo_set, 2 * b + 3)
                    load_xt(b + 1, 1)
                for pair in (2, 3):
                    wait_apart(acc_free, L * b + 2 * pair)
                    load_x(b, pair)
                if next2_xt:
                    wait_apart(xt_lo_set, 2 * b + 4)
                    load_xt(b + 2, 0)
                if next_xt:
                    for pair in (0, 1):
                        wait_apart(acc_free, L * b + 2 * pair + 8)
                        load_x(b + 1, pair)
                for pair in range(TILES // 2):
                    wait_apart(normed, L * b + TILES + 2 * pair + 2)
                    sp.dma_start(out_view[b, :, 2 * pair:2 * pair + 2, :],
                                 x1[:, 2 * pair:2 * pair + 2, :]).then_inc(out_stored[pair], 16)

            sp.dma_start(wq_raw, w_qk[:, 0]).then_inc(wqk_loaded, 16)
            sp.dma_start(xt_raw[:], x_t[0, 0]).then_inc(xt0_loaded, 16)
            sp.dma_start(xt_raw1, x_t[0, 1]).then_inc(xt1_loaded, 16)
            sp.dma_start(p_f[:], w1_t).then_inc(tern_loaded[W1], 16)
            sp.dma_start(wv_raw, w_v).then_inc(wv_loaded, 16)
            sp.dma_start(v_bias[:, 0:D], rows[:, 0:D].broadcast_to([P, D])).then_inc(rows_loaded, 16)
            sp.dma_start(b2_row[:], rows[:, D:].broadcast_to([P, D])).then_inc(rows_loaded, 16)
            sp.wait_ge(wb_psum, 1)
            sp.wait_ge(wv_lo_set, DC)
            sp.dma_start(x1[:], w2_t).then_inc(tern_loaded[W2], 16)
            sp.wait_ge(xt_lo_set, 1)
            load_xt(1, 0)
            sp.wait_ge(xt_lo_set, 2)
            load_x(0, 0)
            load_x(0, 1)
            with sp.Fori(0, B - 2) as b:
                cycle(b, True, True)
            cycle(B - 2, True, False)
            cycle(B - 1, False, False)
            for pair in range(TILES // 2):
                sp.wait_ge(out_stored[pair], 16 * (B + 1))

        @block.tensor
        def _(pe):
            def products(dst, terms, start=True, stop=True):
                for n, (lhs, rhs) in enumerate(terms):
                    last = nc.tensor.matmul(dst, lhs, rhs, start=start and n == 0,
                                            stop=stop and n == len(terms) - 1)
                return last

            def split_terms(l_hi, l_lo, r_hi, r_lo):
                return [(l_lo, r_hi), (l_hi, r_lo), (l_hi, r_hi)]

            def setup():
                pe.wait_ge(const_set, 1)
                for n in range(WARM_UP):
                    products(ps_b[:, 0:P], [(ones[:], ones[:])])
                pe.wait_ge(wqk_loaded, 32)
                for c in range(DC):
                    products(ps_acc[:, c, 0:D], [(wk_raw[:, f, c * P:(c + 1) * P], wq_raw[:, f, :])
                                                 for f in range(DC)]).then_inc(m_psum, 1)
                pe.wait_ge(cols_loaded, 16)
                for c in range(DC):
                    products(ps_a[:, 2 * c:2 * c + 2], [(wq_raw[:, f, c * P:(c + 1) * P], bk_col[:, f, :])
                                                        for f in range(DC)])
                for c in range(DC):
                    products(ps_a[:, 4 + 2 * c:6 + 2 * c], [(wk_raw[:, f, c * P:(c + 1) * P], bq_col[:, f, :])
                                                            for f in range(DC)])
                pe.wait_ge(bqk_set, 1)
                products(ps_a[:, 8:10], [(ones[:], bqk[:, f, :]) for f in range(DC)]).then_inc(wb_psum, 1)

            def abs_total(n):
                pe.wait_ge(acc_free, 2)
                pe.wait_ge(abs_summed, n + 1)
                products(ps_acc[:, n, 0:2], [(ones[:], abs_sum[:, n, :])]).then_inc(abs_psum, 1)

            def g_unit(b, u, first=False):
                half, c = u // DC, u % DC
                pe.wait_ge(xt_lo_set, NH * b + half + 1)
                if first:
                    pe.wait_ge(m_lo_set, DC)
                elif u:
                    pe.wait_ge(g_lo_set, NH * DC * b + u)
                cols = slice(half * HALF, (half + 1) * HALF)
                products(ps_g(u, first), [t for k in range(DC) for t in split_terms(
                    m_hi[:, k, c * P:(c + 1) * P], m_lo[:, k, c * P:(c + 1) * P],
                    xt_hi[:, k, cols], xt_lo[:, k, cols])]).then_inc(g_psum, 1)

            def values(b, j, first):
                rows = slice(j * P, (j + 1) * P)
                if j >= 2:
                    pe.wait_ge(v_taken, TILES * b + j - 1)
                elif j == 0:
                    if first:
                        pe.wait_ge(bias_set, 3)
                        pe.wait_ge(wv_lo_set, DC)
                    else:
                        pe.wait_ge(g_lo_set, NH * DC * (b + 1))
                elif not first:
                    pe.wait_ge(gelu_done, U * b)
                products(ps_v[j % 2][:, 0:DV], [t for k in range(DC) for t in split_terms(
                    xt_hi[:, k, rows], xt_lo[:, k, rows], wv_hi[:, k, :], wv_lo[:, k, :])]).then_inc(v_psum, 1)

            def scores(b, j, first):
                rows = slice(j * P, (j + 1) * P)
                if j >= 2:
                    pe.wait_ge(exp_done, TILES * b + j - 1)
                elif first:
                    pe.wait_ge(g_lo_set, DC * (j + 1))
                for half in range(NH):
                    cols = slice(half * HALF, (half + 1) * HALF)
                    last = products(ps_s[:, (j + 1) % 2, half, :], [t for k in range(DC) for t in split_terms(
                        g_hi[:, k, rows], g_lo[:, k, rows], xt_hi[:, k, cols], xt_lo[:, k, cols])])
                last.then_inc(s_psum, 1)

            def mix_part(b, i, js):
                rows = slice(i * P, (i + 1) * P)
                if 0 in js:
                    pe.wait_ge(acc_free, L * b + i + 1)
                for j in js:
                    if i == 0:
                        pe.wait_ge(p_lo_set, TILES * b + j + 1)
                        pe.wait_ge(v_lo_set, TILES * b + j + 1)
                    wide = (ps_acc[:, i % 2, :], p_hi[:, j, rows], v_hl[:, j, :, :])
                    narrow = (ps_acc[:, i % 2, 0:D], p_lo[:, j, rows], v_hl[:, j, 0, :])
                    for dst, lhs, rhs in ((wide, narrow) if j == 0 else (narrow, wide)):
                        first_of_all, last_of_all = j == 0 and rhs is wide[2], j == TILES - 1 and rhs is wide[2]
                        last = products(dst, [(lhs, rhs)], start=first_of_all, stop=last_of_all)
                if TILES - 1 in js:
                    last.then_inc(acc_psum, 1)

            def mix(b, i):
                mix_part(b, i, range(TILES))

            def mix_pair(b):
                mix_part(b, 0, range(TILES - 1))
                mix_part(b, 1, range(TILES - 4))
                mix_part(b, 0, range(TILES - 1, TILES))
                mix_part(b, 1, range(TILES - 4, TILES))

            def transpose_half(b, half):
                pe.wait_ge(normed, L * b + TPH * (half + 1))
                for c in range(DC):
                    for i in range(TPH):
                        last = nc.tensor.transpose(ps_s[:, 1, c, i * P:(i + 1) * P],
                                                   x1[:, half * TPH + i, c * P:(c + 1) * P], identity[:])
                    last.then_inc(t_psum, 1)

            def up(b, u):
                half, f = u // FC, u % FC
                if f == 0:
                    pe.wait_ge(t_lo_set, DC * (NH * b + half + 1))
                if u == 0:
                    pe.wait_ge(tern_set, TERN_PARTS[W1] + TERN_PARTS[W2])
                if u >= len(ps_h):
                    pe.wait_ge(gelu_done, U * b + u - len(ps_h) + 1)
                products(ps_h[u % len(ps_h)], [(w1[:, k, f * P:(f + 1) * P], part[:, k, :])
                                               for part in (x1t_lo, x1t_hi) for k in range(DC)]).then_inc(h_psum, 1)

            def down(b, t):
                half, cols = t // TPH, slice((t % TPH) * P, (t % TPH + 1) * P)
                pe.wait_ge(acc_free, L * b + TILES + t + 1)
                for f in range(FC):
                    if t % TPH == 0:
                        pe.wait_ge(h_lo_set, U * b + half * FC + f + 1)
                    last = products(ps_acc[:, t % 2, 0:D], [(h_lo[:, f, cols], w2[:, f, :]), (h_hi[:, f, cols], w2[:, f, :])],
                                    start=f == 0, stop=f == FC - 1)
                last.then_inc(acc_psum, 1)

            def attend(b, first=False):
                for j in range(TILES):
                    if first and j == 0:
                        values(b, 0, first)
                        values(b, 1, first)
                    if not first or j >= 2:
                        values(b, j, first)
                    if first and j == 6:
                        abs_total(W2)
                    scores(b, j, first)
                    if first and j == 0:
                        abs_total(W1)
                    if not first and j in DOWN_AFTER:
                        for t in DOWN_AFTER[j]:
                            down(b - 1, t)

            def mix_and_feed(b, last=False):
                def g(u):
                    if not last:
                        g_unit(b + 1, u)
                mix_pair(b); mix(b, 2); g(0)
                mix(b, 3); g(1)
                mix(b, 4); g(2)
                mix(b, 5); transpose_half(b, 0)
                mix(b, 6)
                for u in range(UP_EARLY):
                    up(b, u)
                mix(b, 7); g(3)
                for u in range(UP_EARLY, FC):
                    up(b, u)
                transpose_half(b, 1)
                for t in range(TPH):
                    down(b, t)
                for u in range(FC, U):
                    up(b, u)

            setup()
            for u in range(NH * DC):
                g_unit(0, u, first=True)
            attend(0, first=True)
            with pe.Fori(0, B - 1) as b:
                mix_and_feed(b)
                attend(b + 1)
            mix_and_feed(B - 1, last=True)
            for t in range(TPH, TILES):
                down(B - 1, t)

        @block.scalar
        def _(act):
            def setup():
                act.dma_start(wk_raw, w_qk[:, 1]).then_inc(wqk_loaded, 16)
                act.dma_start(column[:], cols).then_inc(cols_loaded, 16)
                xt_high(0, 0, first=True)
                for c in range(DC):
                    act.wait_ge(m_psum, c + 1)
                    nc.scalar.activation(m_hi[:, c, :], ps_acc[:, c, 0:D], ACT.Copy, scale=SCALE).then_inc(m_hi_set, 1)
                act.wait_ge(wb_psum, 1)
                for c in range(DC):
                    nc.scalar.activation(wv_hi[:, c, D:DV], ps_a[:, 4 + 2 * c:6 + 2 * c], ACT.Copy,
                                         scale=SCALE).then_inc(wb_hi_set, 1)
                xt_high(0, 1, first=True)
                sign(W1)
                g_high(0, 0, first=True)
                act.wait_ge(wv_loaded, 16)
                for c in range(DC):
                    nc.scalar.activation(wv_hi[:, c, 0:D], wv_raw[:, c, :], ACT.Copy).then_inc(wv_hi_set, 1)

            def sign(n):
                act.wait_ge(tern_loaded[n], 16)
                nc.scalar.activation(tern_sign[n], tern_raw[n], ACT.Sign).then_inc(sign_set, 1)

            def sums(n, parts):
                act.wait_ge(sign_set, n + 1)
                size = D * FF // P // PARTS
                for k in parts:
                    part = tern_raw[n][:, k * size:(k + 1) * size]
                    nc.scalar.activation(part, part, ACT.Abs, accum_out=abs_part[:, n, k:k + 1]).then_inc(abs_set, 1)

            def xt_high(b, half, first=False):
                if first:
                    act.wait_ge(xt1_loaded if half else xt0_loaded, 16)
                else:
                    act.wait_ge(xt_loaded, 16 * (NH * (b - 1) + half + 1))
                    act.wait_ge(s_psum, TILES * b)
                raw = xt_raw1 if first and half else xt_raw[:]
                nc.scalar.activation(xt_hi[:, :, half * HALF:(half + 1) * HALF], raw, ACT.Copy).then_inc(xt_hi_set, 1)

            def g_high(b, u, first=False):
                half, c = u // DC, u % DC
                if first:
                    act.wait_ge(bias_set, DC)
                act.wait_ge(g_psum, NH * DC * b + u + 1)
                nc.scalar.activation(g_hi[:, c, half * HALF:(half + 1) * HALF], ps_g(u, first), ACT.Identity,
                                     bias=g_bias[:, c:c + 1]).then_inc(g_hi_set, 1)

            def exponentials(b, j, first):
                if j >= 2:
                    act.wait_ge(p_lo_set, TILES * b + j - 1)
                elif j == 0 and not first:
                    act.wait_ge(h_lo_set, U * b)
                if first and j < 2:
                    act.wait_ge(tern_set, j + 1)
                act.wait_ge(bias_ready, TILES * b + j + 1)
                nc.scalar.activation(p_f[:, j % 2, :], ps_s[:, (j + 1) % 2, :, :], ACT.Exp, bias=s_bias[:, j:j + 1],
                                     accum_out=p_sum[:, j:j + 1]).then_inc(exp_done, 1)

            def p_high(b, j):
                act.wait_ge(exp_done, TILES * b + j + 1)
                nc.scalar.activation(p_hi[:, j, :], p_f[:, j % 2, :], ACT.Copy).then_inc(p_hi_set, 1)

            def v_high(b, j):
                act.wait_ge(rsum_set, TILES * b + j + 1)
                nc.scalar.activation(v_hl[:, j, 0, :], v_f[:, j % 2, 0:D], ACT.Copy,
                                     scale=p_rsum[:, j:j + 1]).then_inc(v_hi_set, 1)

            def normalise(b, k):
                i = k % TILES
                act.wait_ge(shift_set, L * b + k + 1)
                nc.scalar.activation(x1[:, i, :], x1[:, i, :], ACT.Identity, bias=shift[:, k:k + 1],
                                     scale=rstd[:, k:k + 1]).then_inc(normed, 1)

            def t_high(b, half):
                for c in range(DC):
                    act.wait_ge(t_psum, DC * (NH * b + half) + c + 1)
                    if half:
                        act.wait_ge(h_psum, U * b + FC)
                    nc.scalar.activation(x1t_hi[:, c, :], ps_s[:, 1, c, :], ACT.Copy).then_inc(t_hi_set, 1)

            def gelu(b, u):
                act.wait_ge(h_psum, U * b + u + 1)
                if u >= RH:
                    act.wait_ge(h_lo_set, U * b + u - RH + 1)
                nc.scalar.activation(h_f[:, u % RH, :], ps_h[u % len(ps_h)], ACT.Gelu,
                                     bias=b1_col[:, u % FC:u % FC + 1]).then_inc(gelu_done, 1)

            def h_high(b, u):
                act.wait_ge(gelu_done, U * b + u + 1)
                if u >= FC:
                    act.wait_ge(acc_psum, L * b + TILES + TPH)
                nc.scalar.activation(h_hi[:, u % FC, :], h_f[:, u % RH, :], ACT.Copy).then_inc(h_hi_act, 1)

            def gelus(b, units):
                for u in units:
                    gelu(b, u)
                    if u != units[0] and u - 1 in H_HIGH_ACT:
                        h_high(b, u - 1)
                if units[-1] in H_HIGH_ACT:
                    h_high(b, units[-1])

            def attend(b, first=False):
                for j in range(TILES):
                    exponentials(b, j, first)
                    p_high(b, j)
                    v_high(b, j)
                    if first and j in W2_SUMS_AFTER:
                        sums(W2, W2_SUMS_AFTER[j])
                    if not first:
                        for k in {0: [8, 9], 1: [10, 11], 6: [12]}.get(j, []):
                            normalise(b - 1, k)
                if not first:
                    for k in range(L - 3, L):
                        normalise(b - 1, k)

            def mix_and_feed(b, last=False):
                def g(u):
                    if not last:
                        g_high(b + 1, u)

                def n(k):
                    normalise(b, k)

                def x_half(half):
                    if not last:
                        xt_high(b + 1, half)
                x_half(0); n(0); g(0); n(1); n(2); x_half(1); g(1); n(3); g(2)
                n(4); t_high(b, 0)
                n(5); gelus(b, range(UP_EARLY)); n(6)
                g(3); gelus(b, range(UP_EARLY, FC - 2)); n(7); gelus(b, range(FC - 2, FC))
                t_high(b, 1)
                gelus(b, range(FC, U))

            setup()
            g_high(0, 1, first=True)
            g_high(0, 2, first=True)
            sums(W1, range(PARTS))
            g_high(0, 3, first=True)
            sign(W2)
            attend(0, first=True)
            with act.Fori(0, B - 1) as b:
                mix_and_feed(b)
                attend(b + 1)
            mix_and_feed(B - 1, last=True)
            for k in range(TILES, L):
                normalise(B - 1, k)

        @block.vector
        def _(dve):
            def setup():
                nc.vector.memset(ones[:], 1.0).then_inc(const_set, 1)
                nc.vector.memset(neg_half[:], -0.5).then_inc(const_set, 1)
                nc.vector.memset(eps[:], LN_EPS).then_inc(const_set, 1)
                nc.vector.memset(zero[:], 0.0).then_inc(const_set, 1)
                nc.vector.memset(abs_sum[:], 0.0).then_inc(const_set, 1)
                dve.wait_ge(const_set, CONSTS)
                for q in range(TILES // 2):
                    nc.vector.tensor_copy(s_max[:, 2 + q:3 + q], ones[:, 0:1]).then_inc(out_stored[q], 16)
                dve.wait_ge(cols_loaded, 16)
                nc.vector.tensor_tensor(bqk[:], bq_col, bk_col, ALU.mult).then_inc(bqk_set, 1)
                xt_low(0, 0, first=True)
                for c in range(DC):
                    dve.wait_ge(m_hi_set, c + 1)
                    nc.vector.scalar_tensor_tensor(m_lo[:, c, :], ps_acc[:, c, 0:D], SCALE, m_hi[:, c, :].bitcast(F32),
                                                   ALU.mult, ALU.subtract).then_inc(m_lo_set, 1)
                dve.wait_ge(m_lo_set, DC)
                nc.vector.tensor_copy(s_max[:, 0:2], ones[:, 0:2]).then_inc(acc_free, 2)
                dve.wait_ge(wb_hi_set, DC)
                for c in range(DC):
                    nc.vector.tensor_scalar(g_bias[:, c:c + 1], ps_a[:, 2 * c:2 * c + 1], SCALE, None,
                                            ALU.mult).then_inc(bias_set, 1)
                nc.vector.tensor_scalar(v_bias[:, D:DV], ps_a[:, 8:10], SCALE, None, ALU.mult).then_inc(bias_set, 1)

            def values_low():
                dve.wait_ge(wv_hi_set, DC)
                for c in range(DC):
                    nc.vector.scalar_tensor_tensor(wv_lo[:, c, D:DV], ps_a[:, 4 + 2 * c:6 + 2 * c], SCALE,
                                                   wv_hi[:, c, D:DV].bitcast(F32), ALU.mult, ALU.subtract)
                    nc.vector.tensor_tensor(wv_lo[:, c, 0:D], wv_raw[:, c, :], wv_hi[:, c, 0:D].bitcast(F32),
                                            ALU.subtract).then_inc(wv_lo_set, 1)

            def abs_sums(n):
                dve.wait_ge(abs_set, PARTS * (n + 1))
                nc.vector.tensor_reduce(abs_sum[:, n, 0:1], abs_part[:, n, :], AX_X, ALU.add).then_inc(abs_summed, 1)

            def thresholds(n):
                dve.wait_ge(abs_psum, n + 1)
                nc.vector.tensor_scalar(scale[:, n:n + 1], ps_acc[:, n, 0:1], 1.0 / (D * FF), MIN_SCALE,
                                        ALU.mult, ALU.max).then_inc(scale_set, 1)
                dve.wait_ge(scale_set, n + 1)
                nc.vector.tensor_scalar(cut[:, n:n + 1], scale[:, n:n + 1], 0.5, None, ALU.mult).then_inc(cut_set, 1)

            def ternary(n, part):
                dve.wait_ge(cut_set, n + 1)
                size = D * FF // P // TERN_PARTS[n]
                some = slice(part * size, (part + 1) * size)
                nc.vector.scalar_tensor_tensor(tern_out[n][:, some], tern_raw[n][:, some], cut[:, n:n + 1],
                                               tern_sign[n][:, some].bitcast(F32), ALU.is_gt, ALU.mult).then_inc(tern_set, 1)

            def xt_low(b, half, first=False):
                dve.wait_ge(xt_hi_set, NH * b + half + 1)
                cols = slice(half * HALF, (half + 1) * HALF)
                raw = xt_raw1 if first and half else xt_raw[:]
                nc.vector.tensor_tensor(xt_lo[:, :, cols], raw, xt_hi[:, :, cols].bitcast(F32),
                                        ALU.subtract).then_inc(xt_lo_set, 1)

            def g_low(b, u, first=False):
                half, c = u // DC, u % DC
                cols = slice(half * HALF, (half + 1) * HALF)
                dve.wait_ge(g_hi_set, NH * DC * b + u + 1)
                nc.vector.scalar_tensor_tensor(g_lo[:, c, cols], ps_g(u, first), g_bias[:, c:c + 1],
                                               g_hi[:, c, cols].bitcast(F32), ALU.add, ALU.subtract).then_inc(g_lo_set, 1)

            def softmax_sums(b, j):
                dve.wait_ge(exp_done, TILES * b + j + 1)
                nc.vector.reciprocal(p_rsum[:, j:j + 1], p_sum[:, j:j + 1]).then_inc(rsum_set, 1)

            def v_and_max(b, j, first):
                if first and j == 0:
                    dve.wait_ge(rows_loaded, 32)
                dve.wait_ge(v_psum, TILES * b + j + 1)
                if j >= 2 or not first:
                    dve.wait_ge(v_lo_set, TILES * b + max(j - 1, 0))
                nc.vector.tensor_tensor(v_f[:, j % 2, :], ps_v[j % 2][:, 0:DV], v_bias[:], ALU.add).then_inc(v_taken, 1)
                dve.wait_ge(s_psum, TILES * b + j + 1)
                nc.vector.tensor_reduce(s_max[:, j:j + 1], ps_s[:, (j + 1) % 2, :, :].rearrange("p a n -> p (a n)"),
                                        AX_X, ALU.max, negate=True).then_inc(max_set, 1)

            def exp_bias(b, j):
                t = v_f[:, j % 2, D:D + 1]
                dve.wait_ge(v_taken, TILES * b + j + 1)
                dve.wait_ge(max_set, TILES * b + j + 1)
                nc.vector.scalar_tensor_tensor(s_bias[:, j:j + 1], s_max[:, j:j + 1], t, t,
                                               ALU.subtract, ALU.add).then_inc(bias_ready, 1)

            def p_low(b, j):
                dve.wait_ge(p_hi_set, TILES * b + j + 1)
                nc.vector.tensor_tensor(p_lo[:, j, :], p_f[:, j % 2, :], p_hi[:, j, :].bitcast(F32),
                                        ALU.subtract).then_inc(p_lo_set, 1)

            def residual(b, k):
                i = k % TILES
                dve.wait_ge(acc_psum, L * b + k + 1)
                if k < TILES:
                    dve.wait_ge(x_loaded[(i // 2) % 2], 16 * (2 * b + i // 4 + 1))
                    if i % 2 == 0:
                        dve.wait_ge(out_stored[i // 2], 16 * (b + 1))
                    nc.vector.tensor_tensor(x1[:, i, :], ps_acc[:, i % 2, D:], x_tok[:, i % 4, :],
                                            ALU.add).then_inc(low_added, 1)
                    dve.wait_ge(low_added, TILES * b + k + 1)
                elif i % TPH == 0:
                    dve.wait_ge(b2_added, NH * b + i // TPH + 1)
                nc.vector.tensor_tensor(x1[:, i, :], ps_acc[:, i % 2, 0:D], x1[:, i, :], ALU.add).then_inc(acc_free, 1)
                dve.wait_ge(acc_free, L * b + k + 3)
                nc.vector.bn_stats(stats[:, k, :], x1[:, i, :]).then_inc(stats_set, 1)
                dve.wait_ge(const_set, CONSTS)
                dve.wait_ge(stats_set, L * b + k + 1)
                nc.vector.bn_aggr(mean_var[:, k, :], stats[:, k, :]).then_inc(mv_set, 1)

            def t_low(b, half):
                for c in range(DC):
                    dve.wait_ge(t_hi_set, DC * (NH * b + half) + c + 1)
                    nc.vector.tensor_tensor(x1t_lo[:, c, :], ps_s[:, 1, c, :], x1t_hi[:, c, :].bitcast(F32),
                                            ALU.subtract).then_inc(t_lo_set, 1)

            def h_high(b, u):
                dve.wait_ge(gelu_done, U * b + u + 1)
                if u >= FC:
                    dve.wait_ge(acc_psum, L * b + TILES + TPH)
                nc.vector.tensor_copy(h_hi[:, u % FC, :], h_f[:, u % RH, :]).then_inc(h_hi_dve, 1)

            def h_low(b, u):
                f = u % FC
                if u in H_HIGH_ACT:
                    dve.wait_ge(h_hi_act, len(H_HIGH_ACT) * b + len([n for n in H_HIGH_ACT if n <= u]))
                else:
                    dve.wait_ge(h_hi_dve, (U - len(H_HIGH_ACT)) * b + len([n for n in range(u + 1) if n not in H_HIGH_ACT]))
                nc.vector.tensor_tensor(h_lo[:, f, :], h_f[:, u % RH, :], h_hi[:, f, :].bitcast(F32),
                                        ALU.subtract).then_inc(h_lo_set, 1)

            def h_halves(b, units):
                for n, u in enumerate(units):
                    if u not in H_HIGH_ACT:
                        h_high(b, u)
                    if n:
                        h_low(b, u - 1)
                h_low(b, units[-1])

            def attend(b, first=False):
                for j in range(TILES):
                    if j:
                        softmax_sums(b, j - 1)
                    v_and_max(b, j, first)
                    if first and j == 0:
                        thresholds(W1)
                        ternary(W1, 0)
                    exp_bias(b, j)
                    if not first and j == TILES - 1:
                        residual(b - 1, L - 3)
                    if j:
                        p_low(b, j - 1)
                    if first and j == 0:
                        ternary(W1, 1)
                    if first and j == 4:
                        abs_sums(W2)
                    if first and j == 6:
                        thresholds(W2)
                        ternary(W2, 0)
                    if not first and j in DOWN_AFTER and j < TILES - 1:
                        for t in DOWN_AFTER[j]:
                            residual(b - 1, TILES + t)
                softmax_sums(b, TILES - 1)
                if first:
                    ternary(W2, 1)
                else:
                    residual(b - 1, L - 2)
                p_low(b, TILES - 1)
                if first:
                    ternary(W2, 2)
                    ternary(W2, 3)
                    dve.wait_ge(tern_set, TERN_PARTS[W1] + TERN_PARTS[W2])
                else:
                    residual(b - 1, L - 1)

            def mix_and_feed(b, last=False):
                def g(u):
                    if not last:
                        g_low(b + 1, u)

                def r(k):
                    residual(b, k)

                def x_half(half):
                    if not last:
                        xt_low(b + 1, half)
                r(0); x_half(0); r(1); r(2); g(0); r(3); x_half(1); g(1); r(4); g(2)
                r(5); t_low(b, 0)
                r(6); h_halves(b, range(UP_EARLY)); r(7); g(3); h_halves(b, range(UP_EARLY, FC))
                t_low(b, 1)
                r(8); r(9); r(10); r(11)
                h_halves(b, range(FC, U))

            setup()
            xt_low(0, 1, first=True)
            g_low(0, 0, first=True)
            values_low()
            g_low(0, 1, first=True)
            g_low(0, 2, first=True)
            abs_sums(W1)
            g_low(0, 3, first=True)
            attend(0, first=True)
            with dve.Fori(0, B - 1) as b:
                mix_and_feed(b)
                attend(b + 1)
            mix_and_feed(B - 1, last=True)
            for t in range(TPH, TILES):
                residual(B - 1, TILES + t)

        @block.gpsimd
        def _(pool):
            def v_low(b, j, first):
                pool.wait_ge(rsum_set, TILES * b + j + 1)
                if not (first and j == 0):
                    pool.wait_ge(v_lo_set, TILES * b + j)
                nc.gpsimd.tensor_tensor(v_scaled[:], v_f[:, j % 2, 0:D], p_rsum[:, j:j + 1].broadcast_to([P, D]),
                                        ALU.mult).then_inc(v_scaled_set, 1)
                pool.wait_ge(v_hi_set, TILES * b + j + 1)
                pool.wait_ge(v_scaled_set, TILES * b + j + 1)
                nc.gpsimd.tensor_tensor(v_hl[:, j, 1, :], v_scaled[:], v_hl[:, j, 0, :].bitcast(F32),
                                        ALU.subtract).then_inc(v_lo_set, 1)

            def norm_factors(b, k):
                pool.wait_ge(mv_set, L * b + k + 1)
                nc.gpsimd.tensor_tensor(var_eps[:, k:k + 1], mean_var[:, k, 1:2], eps[:], ALU.add)
                nc.gpsimd.tensor_tensor(neg_mean[:, k:k + 1], zero[:], mean_var[:, k, 0:1], ALU.subtract).then_inc(eps_set, 1)
                pool.wait_ge(eps_set, L * b + k + 1)
                nc.gpsimd.tensor_tensor(rstd[:, k:k + 1], var_eps[:, k:k + 1], neg_half[:], ALU.pow).then_inc(rstd_set, 1)
                pool.wait_ge(rstd_set, L * b + k + 1)
                nc.gpsimd.tensor_tensor(shift[:, k:k + 1], neg_mean[:, k:k + 1], rstd[:, k:k + 1],
                                        ALU.mult).then_inc(shift_set, 1)

            def add_b2(b, half):
                pool.wait_ge(t_psum, DC * (NH * b + half + 1))
                tiles = x1[:, half * TPH:(half + 1) * TPH, :]
                nc.gpsimd.tensor_tensor(tiles, tiles, b2_row[:].unsqueeze(1).broadcast_to([P, TPH, D]),
                                        ALU.add).then_inc(b2_added, 1)

            def mix_and_feed(b):
                for k in range(6):
                    norm_factors(b, k)
                add_b2(b, 0)
                for k in range(6, 8):
                    norm_factors(b, k)
                add_b2(b, 1)
                for k in range(8, 12):
                    norm_factors(b, k)

            def attend(b, first=False):
                for j in range(TILES):
                    v_low(b, j, first)
                    if not first and j == 3:
                        norm_factors(b - 1, L - 4)
                    if not first and j == 6:
                        norm_factors(b - 1, L - 3)
                if not first:
                    norm_factors(b - 1, L - 2)
                    norm_factors(b - 1, L - 1)

            pool.wait_ge(const_set, CONSTS)
            attend(0, first=True)
            pool.wait_ge(rows_loaded, 32)
            with pool.Fori(0, B - 1) as b:
                mix_and_feed(b)
                attend(b + 1)
            mix_and_feed(B - 1)
            for k in range(L - 4, L):
                norm_factors(B - 1, k)


_INS = ["x", "x_t", "w_qk", "w_v", "cols", "rows", "w1_t", "w2_t"]


def kernel(L0_attn_x, L0_attn_W, L0_attn_b, L0_ffn_W1, L0_ffn_b1, L0_ffn_W2, L0_ffn_b2):
    import numpy as np
    import concourse.bacc as bacc
    from concourse import mybir as _mybir
    from concourse.bass_utils import run_bass_kernel_spmd as run

    x, W, b, W1, b1, W2, b2 = (np.asarray(a) for a in (
        L0_attn_x, L0_attn_W, L0_attn_b, L0_ffn_W1, L0_ffn_b1, L0_ffn_W2, L0_ffn_b2))
    B, S, D = x.shape
    FF = W1.shape[0]
    DC, FC, TILES, NH = D // P, FF // P, S // P, S // HALF

    def column(v):
        return np.stack([v.reshape(DC, P).T, np.zeros((P, DC), v.dtype)], axis=-1).reshape(P, 2 * DC)

    arrays = {
        "x": x,
        "x_t": x.reshape(B, P, NH, TILES // NH, DC, P).transpose(0, 2, 5, 4, 3, 1).reshape(B, NH, P, DC, HALF),
        "w_qk": W[:2 * D].reshape(2, DC, P, D).transpose(2, 0, 1, 3),
        "w_v": W[2 * D:].T.reshape(DC, P, D).transpose(1, 0, 2),
        "cols": np.concatenate([column(b[:D]), column(b[D:2 * D]), b1.reshape(FC, P).T,
                                np.eye(P, dtype=x.dtype)], axis=1),
        "rows": np.concatenate([b[2 * D:], b2]).reshape(1, 2 * D),
        "w1_t": W1.T.reshape(DC, P, FF).transpose(1, 0, 2),
        "w2_t": W2.T.reshape(FC, P, D).transpose(1, 0, 2),
    }
    arrays = {n: np.ascontiguousarray(a) for n, a in arrays.items()}
    nc = bacc.Bacc("TRN2", target_bir_lowering=False, num_devices=1)
    args = [nc.dram_tensor(f"in_{n}", arrays[n].shape, _mybir.dt.from_np(arrays[n].dtype),
                           kind="ExternalInput").ap() for n in _INS]
    out = nc.dram_tensor("out_0", x.shape, _mybir.dt.from_np(x.dtype), kind="ExternalOutput").ap()
    postln_block_kernel(nc, *args, out)
    r = run(nc, [{f"in_{n}": arrays[n] for n in _INS}], core_ids=[0])
    return r.results[0]["out_0"]
```
